# Optimizing a Trainium2 kernel written in Bass

```python
import numpy as np
import jax
import jax.numpy as jnp

def _softmax(x, axis=-1):
    return jax.nn.softmax(x, axis=axis)

def _gelu(x):
    return jax.nn.gelu(x, approximate=True)

def _silu(x):
    return jax.nn.silu(x)

def _sigmoid(x):
    return jax.nn.sigmoid(x)

def _layernorm(x, axis=-1, eps=1e-05):
    m = jnp.mean(x, axis=axis, keepdims=True)
    v = jnp.var(x, axis=axis, keepdims=True)
    return (x - m) / jnp.sqrt(v + eps)

def _scatter_add(tgt, idx, src, axis=0):
    return tgt.at[idx].add(src)

def _segment_sum(src, seg, n):
    return jax.ops.segment_sum(src, seg, n)
kernel_name = 'mk_xattn_ffn_d1_seqx_r4_78f309'

def setup_inputs(seed: int=0):
    np.random.seed(seed)
    _w = jnp.asarray

    def _rec_inputs():
        import jax
        import jax.numpy as jnp
        _rk = jax.random.key(seed)
        x = 7.22e-05 + 1 * jax.random.normal(jax.random.fold_in(_rk, 1), (8, 256, 256), jnp.float32)
        _lenS = 256 - jax.random.randint(jax.random.fold_in(_rk, 7), (8,), 0, max(1, 256 // 4) + 1, jnp.int32)
        _lenS2 = 256 - jax.random.randint(jax.random.fold_in(_rk, 8), (8,), 0, max(1, 256 // 4) + 1, jnp.int32)
        _ctx_1024P = jax.random.normal(jax.random.fold_in(_rk, 11), (8, 16, 256), jnp.float32)
        _ctx_1024c = jax.random.dirichlet(jax.random.fold_in(_rk, 511), 0.3 * jnp.ones((16,), jnp.float32), (8, 256))
        _ctx_1024t = jnp.einsum('bsk,bkd->bsd', _ctx_1024c, _ctx_1024P)
        _ctx_1024t = _ctx_1024t * jax.lax.rsqrt(jnp.mean(jnp.square(_ctx_1024t)) + 1e-12) * 0.953939
        ctx_1024 = 4.13588e-05 + 0.999923 * (_ctx_1024t + 0.3 * jax.random.normal(jax.random.fold_in(_rk, 611), (8, 256, 256), jnp.float32))
        return (x, ctx_1024)
    x, ctx_1024 = _rec_inputs()

    def _L0_xattn_setup():
        import jax, jax.numpy as jnp
        import numpy as np
        D_MODEL = 256
        key = jax.random.key(seed)
        ks = jax.random.split(key, 11)
        B, S, D = (4, 512, D_MODEL)
        scale = 1.0 / np.sqrt(D)
        inp = {'query': jax.random.normal(ks[0], (B, S, D), dtype=jnp.float32), 'key': jax.random.normal(ks[1], (B, S, D), dtype=jnp.float32), 'value': jax.random.normal(ks[2], (B, S, D), dtype=jnp.float32), 'Wq': jax.random.normal(ks[3], (D, D), dtype=jnp.float32) * scale, 'bq': jnp.zeros((D,), dtype=jnp.float32), 'Wk': jax.random.normal(ks[4], (D, D), dtype=jnp.float32) * scale, 'bk': jnp.zeros((D,), dtype=jnp.float32), 'Wv': jax.random.normal(ks[5], (D, D), dtype=jnp.float32) * scale, 'bv': jnp.zeros((D,), dtype=jnp.float32), 'Wo': jax.random.normal(ks[6], (D, D), dtype=jnp.float32) * scale, 'bo': jnp.zeros((D,), dtype=jnp.float32)}
        return inp
    _L0_xattn_all = _L0_xattn_setup()
    _L0_xattn_in = {k: v for k, v in _L0_xattn_all.items() if k in ('Wq', 'bq', 'Wk', 'bk', 'Wv', 'bv', 'Wo', 'bo')}
    del _L0_xattn_all

    def _L0_ffn_setup():
        import jax, jax.numpy as jnp
        import numpy as np
        NUM_EXPERTS = 8
        TOP_K = 2
        MOE_DIM = 512

        def _moe_forward(x, moe_router, moe_w13, moe_w2):
            b, s, d = x.shape
            x_flat = x.reshape(b * s, d)
            router_logits = jnp.einsum('td,de->te', x_flat, moe_router)
            topk_logits, topk_idx = jax.lax.top_k(router_logits, TOP_K)
            topk_weights = jax.nn.softmax(topk_logits, axis=-1).astype(x.dtype)
            tokens = x_flat.shape[0]
            expert_ids = topk_idx.reshape(tokens * TOP_K)
            dispatch_weights = topk_weights.reshape(tokens * TOP_K)
            sort_idx = jnp.argsort(expert_ids, axis=0)
            token_ids = jnp.arange(tokens * TOP_K, dtype=jnp.int32) // TOP_K
            token_ids_sort = token_ids[sort_idx]
            x_sort = x_flat[token_ids_sort]
            w_sort = dispatch_weights[sort_idx].astype(x_flat.dtype)
            group_sizes = jnp.bincount(expert_ids, length=NUM_EXPERTS).astype(jnp.int32)
            w13_out = jax.lax.ragged_dot(x_sort, moe_w13, group_sizes)
            gate, up = jnp.split(w13_out, [MOE_DIM], axis=-1)
            hidden = jax.nn.silu(gate) * up
            out_dispatch = jax.lax.ragged_dot(hidden, moe_w2, group_sizes)
            out_flat = jnp.zeros_like(x_flat).at[token_ids_sort].add(out_dispatch * w_sort[:, None], mode='drop')
            return out_flat.reshape(b, s, d)
        key = jax.random.key(seed)
        k1, k2, k3, k4 = jax.random.split(key, 4)
        B, S, D = (4, 512, 256)
        x = jax.random.normal(k1, (B, S, D), dtype=jnp.float32)
        moe_router = jax.random.normal(k2, (D, NUM_EXPERTS), dtype=jnp.float32) * 0.02
        moe_w13 = jax.random.normal(k3, (NUM_EXPERTS, D, 2 * MOE_DIM), dtype=jnp.float32) * 0.02
        moe_w2 = jax.random.normal(k4, (NUM_EXPERTS, MOE_DIM, D), dtype=jnp.float32) * 0.02
        return {'x': x, 'moe_router': moe_router, 'moe_w13': moe_w13, 'moe_w2': moe_w2}
    _L0_ffn_all = _L0_ffn_setup()
    _L0_ffn_in = {k: v for k, v in _L0_ffn_all.items() if k in ('moe_router', 'moe_w13', 'moe_w2')}
    del _L0_ffn_all
    return {'x': x, 'ctx_1024': ctx_1024, 'L0_xattn_Wq': _L0_xattn_in['Wq'], 'L0_xattn_bq': _L0_xattn_in['bq'], 'L0_xattn_Wk': _L0_xattn_in['Wk'], 'L0_xattn_bk': _L0_xattn_in['bk'], 'L0_xattn_Wv': _L0_xattn_in['Wv'], 'L0_xattn_bv': _L0_xattn_in['bv'], 'L0_xattn_Wo': _L0_xattn_in['Wo'], 'L0_xattn_bo': _L0_xattn_in['bo'], 'L0_ffn_moe_router': _L0_ffn_in['moe_router'], 'L0_ffn_moe_w13': _L0_ffn_in['moe_w13'], 'L0_ffn_moe_w2': _L0_ffn_in['moe_w2']}

def reference(x, ctx_1024, L0_xattn_Wq, L0_xattn_bq, L0_xattn_Wk, L0_xattn_bk, L0_xattn_Wv, L0_xattn_bv, L0_xattn_Wo, L0_xattn_bo, L0_ffn_moe_router, L0_ffn_moe_w13, L0_ffn_moe_w2):
    import jax
    import jax.numpy as jnp

    def _L0_xattn_ref(query, key, value, Wq, bq, Wk, bk, Wv, bv, Wo, bo):
        import jax, jax.numpy as jnp
        import numpy as np
        D_MODEL = 256
        d_model = query.shape[-1]
        q = jnp.einsum('bsd,ed->bse', query, Wq) + bq
        k = jnp.einsum('bsd,ed->bse', key, Wk) + bk
        v = jnp.einsum('bsd,ed->bse', value, Wv) + bv
        scores = jnp.einsum('bqe,bke->bqk', q, k) / jnp.sqrt(jnp.asarray(d_model, q.dtype))
        attn = jax.nn.softmax(scores, axis=-1)
        out = jnp.einsum('bqk,bke->bqe', attn, v)
        out = jnp.einsum('bqe,fe->bqf', out, Wo) + bo
        return out

    def _L0_ffn_ref(x, moe_router, moe_w13, moe_w2):
        import jax, jax.numpy as jnp
        import numpy as np
        NUM_EXPERTS = 8
        TOP_K = 2
        MOE_DIM = 512

        def _moe_forward(x, moe_router, moe_w13, moe_w2):
            b, s, d = x.shape
            x_flat = x.reshape(b * s, d)
            router_logits = jnp.einsum('td,de->te', x_flat, moe_router)
            topk_logits, topk_idx = jax.lax.top_k(router_logits, TOP_K)
            topk_weights = jax.nn.softmax(topk_logits, axis=-1).astype(x.dtype)
            tokens = x_flat.shape[0]
            expert_ids = topk_idx.reshape(tokens * TOP_K)
            dispatch_weights = topk_weights.reshape(tokens * TOP_K)
            sort_idx = jnp.argsort(expert_ids, axis=0)
            token_ids = jnp.arange(tokens * TOP_K, dtype=jnp.int32) // TOP_K
            token_ids_sort = token_ids[sort_idx]
            x_sort = x_flat[token_ids_sort]
            w_sort = dispatch_weights[sort_idx].astype(x_flat.dtype)
            group_sizes = jnp.bincount(expert_ids, length=NUM_EXPERTS).astype(jnp.int32)
            w13_out = jax.lax.ragged_dot(x_sort, moe_w13, group_sizes)
            gate, up = jnp.split(w13_out, [MOE_DIM], axis=-1)
            hidden = jax.nn.silu(gate) * up
            out_dispatch = jax.lax.ragged_dot(hidden, moe_w2, group_sizes)
            out_flat = jnp.zeros_like(x_flat).at[token_ids_sort].add(out_dispatch * w_sort[:, None], mode='drop')
            return out_flat.reshape(b, s, d)
        return _moe_forward(x, moe_router, moe_w13, moe_w2)
    x = x + _L0_xattn_ref(_layernorm(x, axis=-1), ctx_1024, ctx_1024, L0_xattn_Wq, L0_xattn_bq, L0_xattn_Wk, L0_xattn_bk, L0_xattn_Wv, L0_xattn_bv, L0_xattn_Wo, L0_xattn_bo)
    x = x + _L0_ffn_ref(_layernorm(x, axis=-1), L0_ffn_moe_router, L0_ffn_moe_w13, L0_ffn_moe_w2)
    return x

_drawn_inputs = setup_inputs


def setup_inputs(seed=0):
    import zlib

    import numpy as np

    out = dict(_drawn_inputs(seed))
    spreads = {'L0_xattn_bq': (0.0, 0.451),
     'L0_xattn_bk': (0.0, 0.8),
     'L0_xattn_bv': (0.0, 0.1),
     'L0_xattn_bo': (0.0, 0.1)}
    factors = {'L0_ffn_moe_router': 4.456, 'L0_ffn_moe_w13': 3.799, 'L0_ffn_moe_w2': 3.81}
    for name, (base, spread) in spreads.items():
        noise = np.random.default_rng([zlib.crc32(name.encode()), seed]).standard_normal(out[name].shape)
        drawn = base * np.exp(spread * noise) if base else spread * noise
        out[name] = jnp.asarray(drawn.astype(out[name].dtype))
    for name, factor in factors.items():
        out[name] = (out[name] * factor).astype(out[name].dtype)
    return out
```

```python
from contextlib import ExitStack

import concourse.bass as bass
from concourse import mybir

F32 = mybir.dt.float32
BF16 = mybir.dt.bfloat16
I32 = mybir.dt.int32
U32 = mybir.dt.uint32
ALU = mybir.AluOpType
ACT = mybir.ActivationFunctionType
AX_X = mybir.AxisListType.X

P = 128
EPS = 1e-5
TOP = 2


def at_least(engine, semaphore, count):
    if not (isinstance(count, int) and count <= 0):
        engine.wait_ge(semaphore, count)


def own(engine, semaphore):
    engine.sem_inc(semaphore, 1)


def xattn_moe(nc, x, ctx_in, wq, bq, wk, bk, wv, bv, wo, bo, router, w13, w2, out):
    B, S, D = x.shape
    NE, _, F2 = w13.shape
    F = F2 // 2
    T = B * S
    KD = D // P
    KF = F // P
    NS = S // P
    NBLK = (TOP * T + NE * (P - 1)) // P
    NMETA = NBLK + 1
    ROWS = NE * T
    SCALE = float(D) ** -0.5
    assert KD == 2 and NS == 2 and S == 256 and F == 512 and out.shape[0] == T + P

    xn_dram = nc.dram_tensor("xn_dram", (T + P, D), F32).ap()
    table = nc.dram_tensor("token_table", (ROWS + P, 2), I32).ap()

    with ExitStack() as ctx:
        def sb(name, shape, dt=F32):
            return ctx.enter_context(nc.sbuf_tensor(name, shape, dt))

        def bank(name):
            return ctx.enter_context(nc.psum_tensor(name, [P, 512], F32))

        def sem(name):
            return ctx.enter_context(nc.semaphore(name))

        w13_sb = sb("w13_sb", [P, NE * KD * F2])
        w2_sb = sb("w2_sb", [P, NE * KF * D])

        ident = sb("ident", [P, P])
        ones_f = sb("ones_f", [P, P])
        zero_f = sb("zero_f", [P, D])
        before = sb("before", [P, P], BF16)
        ones_b = sb("ones_b", [P, P], BF16)
        expert_no = sb("expert_no", [P, NS, TOP, NE])
        expert_row = sb("expert_row", [P, NS, NE])
        block_edge = sb("block_edge", [P, NE, T // P])
        block_no = sb("block_no", [P, NMETA, NE])
        minus_half = sb("minus_half", [P, NS])
        spare = sb("spare", [P, P, 2], I32)

        wq_sb = sb("wq_sb", [P, KD, D])
        wk_sb = sb("wk_sb", [P, KD, D])
        wv_sb = sb("wv_sb", [P, KD, D])
        wo_sb = sb("wo_sb", [P, KD, D])
        woT = sb("woT", [P, KD, D])
        bT = sb("bT", [P, KD, D])
        mvo = sb("mvo", [P, KD, D])
        router_sb = sb("router_sb", [P, KD, NE])
        bias_col = sb("bias_col", [P, 3, KD])
        bo_row = sb("bo_row", [1, D])
        bq_wide = sb("bq_wide", [P, KD, P])
        bv_wide = sb("bv_wide", [P, KD, P])
        small = sb("small", [P, 2 * KD + 1])
        bvo = sb("bvo", [P, D])

        x_all = sb("x_all", [P, B, NS, D])
        c_all = sb("c_all", [P, B, NS, D])
        c_turn = sb("c_turn", [P, NS, D])
        c_val = sb("c_val", [P, NS, D])
        xn = sb("xn", [P, NS, D])
        xnT = sb("xnT", [P, KD, S])
        cT = sb("cT", [P, KD, S])
        qT = sb("qT", [P, KD, S])
        probs = sb("probs", [P, NS, S])
        pT = sb("pT", [P, NS, S])
        zT = sb("zT", [P, KD, S])
        xb = sb("xb", [P, NS, D])
        x1 = sb("x1", [P, NS, D])
        xn2 = sb("xn2", [P, NS, D])
        x2T = sb("x2T", [P, KD, S])
        st = sb("st", [P, 2, NS, 6])
        mv = sb("mv", [P, 2, NS, 2])
        rstd = sb("rstd", [P, 2, NS])
        var_eps = sb("var_eps", [P, 2, NS])
        smax = sb("smax", [P, NS])
        full_max = sb("full_max", [P, NS])
        shift = sb("shift", [P, NS])
        nbias = sb("nbias", [P, NS])
        rowsum = sb("rowsum", [P, NS])
        rinv = sb("rinv", [P, NS])
        qbk = sb("qbk", [P, NS])

        logits = sb("logits", [P, NS, NE])
        top_v = sb("top_v", [P, NS, 8])
        top_i = sb("top_i", [P, NS, 8], U32)
        top_f = sb("top_f", [P, NS, TOP])
        onehot = sb("onehot", [P, NS, TOP, NE])
        member = sb("member", [P, NS, NE], BF16)
        so_far = sb("so_far", [P, NE], BF16)
        pos = sb("pos", [P, NS, NE])
        picked = sb("picked", [P, NS, TOP, NE])
        slot_f = sb("slot_f", [P, NS, TOP])
        slot = sb("slot", [P, NS, TOP], I32)
        gap = sb("gap", [P, NS])
        egap = sb("egap", [P, NS])
        egap1 = sb("egap1", [P, NS])
        entry = sb("entry", [P, NS, TOP, 2], I32)
        entry_f = entry[:].bitcast(F32)

        cnt = sb("cnt", [P, NE])
        over = sb("over", [P, NE, T // P])
        nblk = sb("nblk", [P, NE])
        ends = sb("ends", [P, NE])
        done = sb("done", [P, NMETA, NE])
        done_n = sb("done_n", [P, NMETA, NE])
        blk_e = sb("blk_e", [P, NMETA])
        blk_s = sb("blk_s", [P, NMETA])
        blk_j = sb("blk_j", [P, NMETA])
        blk_r = sb("blk_r", [P, NMETA])
        meta = sb("meta", [P, 2, NMETA], I32)

        tab_g = sb("tab_g", [P, 2, 2], I32)
        tab_s = sb("tab_s", [P, 2, 2], I32)
        xg = sb("xg", [P, 2, D])
        xgT = sb("xgT", [P, KD, P])
        sg = sb("sg", [P, F])
        h = sb("h", [P, F])
        hT = sb("hT", [P, KF, P])
        y = sb("y", [P, 2, D])

        banks = [bank(f"bank{n}") for n in range(8)]
        X, C, Q, SC, PT, Z, O, M = banks
        G, U, XG, HT, Y = banks[:5]

        s_wq, s_wk, s_wv, s_wo, s_small = (sem(f"s_{n}") for n in ("wq", "wk", "wv", "wo", "small"))
        s_x0, s_xr, s_c0, s_cr = (sem(f"s_{n}") for n in ("x0", "xr", "c0", "cr"))
        s_dve_here, s_pool_here = sem("s_dve_here"), sem("s_pool_here")
        s_w13, s_w2 = sem("s_w13"), sem("s_w2")
        s_zeroed, s_filled = sem("s_zeroed"), sem("s_filled")
        s_const, s_pre, s_wide, s_spare = (sem(f"s_{n}") for n in ("const", "pre", "wide", "spare"))
        s_fold, s_folded = sem("s_fold"), sem("s_folded")
        s_xn, s_xnT, s_XT, s_CT, s_cT, s_cturn, s_cval = (
            sem(f"s_{n}") for n in ("xn", "xnT", "XT", "CT", "cT", "cturn", "cval"))
        s_Q, s_qT, s_QB, s_qbk, s_S, s_max, s_nb, s_exp, s_rinv = (
            sem(f"s_{n}") for n in ("Q", "qT", "QB", "qbk", "S", "max", "nb", "exp", "rinv"))
        s_PT, s_pT, s_Z, s_zT, s_O, s_x1, s_xb = (
            sem(f"s_{n}") for n in ("PT", "pT", "Z", "zT", "O", "x1", "xb"))
        s_st1, s_ve1, s_rs1, s_st2, s_ve2, s_rs2, s_xn2, s_X2, s_x2T = (
            sem(f"s_{n}") for n in ("st1", "ve1", "rs1", "st2", "ve2", "rs2", "xn2", "X2", "x2T"))
        s_bn1, s_bn2 = sem("s_bn1"), sem("s_bn2")
        s_store_x1, s_store_xn = sem("s_store_x1"), sem("s_store_xn")
        s_L, s_log, s_topv, s_topi, s_topf, s_gap, s_egap, s_eg1, s_hot, s_mem, s_acc = (
            sem(f"s_{n}") for n in ("L", "log", "topv", "topi", "topf", "gap", "egap", "eg1", "hot", "mem", "acc"))
        s_POS, s_pos, s_pick, s_slotf, s_slot, s_w0, s_w1, s_tok, s_scat = (
            sem(f"s_{n}") for n in ("POS", "pos", "pick", "slotf", "slot", "w0", "w1", "tok", "scat"))
        s_CNT, s_m, s_meta = sem("s_CNT"), sem("s_m"), sem("s_meta")
        s_tabg = [sem(f"s_tabg{n}") for n in range(2)]
        s_tabs = [sem(f"s_tabs{n}") for n in range(2)]
        s_gath = [sem(f"s_gath{n}") for n in range(2)]
        s_XG, s_xgT, s_G, s_U, s_silu, s_h, s_HT, s_hT, s_Y, s_y, s_add = (
            sem(f"s_{n}") for n in ("XG", "xgT", "G", "U", "silu", "h", "HT", "hT", "Y", "y", "add"))

        x_v = x.rearrange("b (s p) d -> p b s d", p=P)
        c_v = ctx_in.rearrange("b (s p) d -> p b s d", p=P)
        rows_v = out[0:T].rearrange("(b s p) d -> b p s d", p=P, s=NS)
        xn_v = xn_dram[0:T].rearrange("(b s p) d -> b p s d", p=P, s=NS)

        def part(i):
            if not isinstance(i, int):
                return True, True, True, True
            return -1 <= i < B - 1, 0 <= i < B, 1 <= i <= B, 2 <= i <= B + 1

        def batches(engine, step):
            for i in range(-1, 3):
                step(i)
            with engine.Fori(3, B - 2) as i:
                step(i)
            for i in range(B - 2, B + 2):
                step(i)

        def blocks(engine, step):
            for b in range(3):
                step(0, b)
            with engine.Fori(1, (NBLK - 3) // 2) as j:
                step(j, 1)
                step(j, 2)
            for b in range(NBLK - 2, NBLK + 1):
                step(0, b)

        assert NBLK % 2 == 1

        block = ctx.enter_context(nc.Block())

        @block.sync
        def _(sp):
            def kp(w):
                return w.rearrange("(k p) d -> p k d", p=P)

            sp.dma_start(x_all[:, 0], x_v[:, 0]).then_inc(s_x0, 16)
            sp.dma_start(wq_sb[:], kp(wq)).then_inc(s_wq, 16)
            sp.dma_start(wk_sb[:], kp(wk)).then_inc(s_wk, 16)
            sp.dma_start(c_all[:, 0], c_v[:, 0]).then_inc(s_c0, 16)
            with nc.allow_non_contiguous_dma("three bias vectors turned into columns"):
                for n, b in enumerate((bq, bk, bv)):
                    sp.dma_start(bias_col[:, n, :], b.rearrange("(k p) -> p k", p=P)).then_inc(s_small, 16)
            sp.dma_start(bo_row[0:1, :], bo.rearrange("(a d) -> a d", a=1)).then_inc(s_small, 16)
            sp.dma_start(router_sb[:], kp(router)).then_inc(s_small, 16)
            sp.dma_start(wo_sb[:], kp(wo)).then_inc(s_wo, 16)
            sp.dma_start(wv_sb[:], kp(wv)).then_inc(s_wv, 16)
            sp.dma_start(x_all[:, 1:B], x_v[:, 1:B]).then_inc(s_xr, 16)
            sp.dma_start(c_all[:, 1:B], c_v[:, 1:B]).then_inc(s_cr, 16)
            sp.wait_ge(s_pre, 1)
            sp.dma_start(xn_dram[T:T + P], zero_f[:]).then_inc(s_zeroed, 16)
            sp.dma_start(out[T:T + P], zero_f[:]).then_inc(s_zeroed, 16)
            sp.wait_ge(s_spare, 2)
            sp.dma_start(table[0:ROWS].rearrange("(p c) w -> p (c w)", p=P),
                         spare[:].rearrange("p c w -> p (c w)")).then_inc(s_filled, 16)
            sp.dma_start(table[ROWS:ROWS + P].rearrange("(a c) w -> a (c w)", a=1),
                         spare[0:1].rearrange("p c w -> p (c w)")).then_inc(s_filled, 16)

            def store(i):
                if part(i)[2]:
                    p = i - 1
                    sp.wait_ge(s_x1, p + 1)
                    sp.dma_start(rows_v[p], x1[:]).then_inc(s_store_x1, 16)
                    sp.wait_ge(s_xn2, p + 1)
                    sp.dma_start(xn_v[p], xn2[:]).then_inc(s_store_xn, 16)

            batches(sp, store)

            def first_row(j, c):
                return sp.value_load(meta[0:1, 1, bass.ds(2 * j + c, 1)], min_val=0, max_val=ROWS)

            def rows_gather(j, c):
                r = first_row(j, c)
                sp.dma_start(tab_g[:, c % 2, :], table[bass.ds(r, P), :]).then_inc(s_tabg[c % 2], 16)

            def rows_scatter(j, c):
                r = first_row(j, c)
                sp.dma_start(tab_s[:, c % 2, :], table[bass.ds(r, P), :]).then_inc(s_tabs[c % 2], 16)

            sp.wait_ge(s_meta, 1)
            sp.wait_ge(s_scat, 16 * B * NS * TOP)
            rows_gather(0, 0)
            rows_gather(0, 1)

            def load_rows(j, c):
                b = 2 * j + c
                if not isinstance(b, int) or b + 2 < NBLK:
                    sp.wait_ge(s_gath[c % 2], 16 * (j + c // 2 + 1))
                    rows_gather(j, c + 2)
                if not isinstance(b, int) or b < NBLK:
                    at_least(sp, s_add, 16 * (b - 1))
                    rows_scatter(j, c)

            blocks(sp, load_rows)
            sp.wait_ge(s_add, 16 * NBLK)
            sp.wait_ge(s_store_x1, 16 * B)
            sp.wait_ge(s_zeroed, 32)

        @block.scalar
        def _(act):
            act.wait_ge(s_fold, 1)
            nc.scalar.activation(woT[:].rearrange("p k d -> p (k d)"), PT[:], ACT.Copy).then_inc(s_folded, 1)
            act.wait_ge(s_fold, 2)
            nc.scalar.activation(bT[:].rearrange("p k d -> p (k d)"), Z[:], ACT.Copy).then_inc(s_folded, 1)
            act.wait_ge(s_fold, 3)
            nc.scalar.activation(small[:], M[:, 0:2 * KD + 1], ACT.Copy).then_inc(s_folded, 1)
            act.wait_ge(s_fold, 4)
            nc.scalar.activation(mvo[:].rearrange("p k d -> p (k d)"), SC[:], ACT.Copy).then_inc(s_folded, 1)
            act.wait_ge(s_fold, 5)
            nc.scalar.activation(bvo[:], O[:, 0:D], ACT.Copy).then_inc(s_folded, 1)
            act.wait_ge(s_folded, 5)
            for e in range(NE):
                act.dma_start(
                    w13_sb[:, e * KD * F2:(e + 1) * KD * F2].rearrange("p (k f) -> p k f", k=KD),
                    w13[e].rearrange("(k p) f -> p k f", p=P)).then_inc(s_w13, 16)
            for e in range(NE):
                act.dma_start(
                    w2_sb[:, e * KF * D:(e + 1) * KF * D].rearrange("p (k d) -> p k d", k=KF),
                    w2[e].rearrange("(k p) d -> p k d", p=P)).then_inc(s_w2, 16)

            def step(i):
                nxt, cur, prev, prev2 = part(i)
                n, p, pp = i + 1, i - 1, i - 2
                if nxt:
                    act.wait_ge(s_XT, n + 1)
                    nc.scalar.activation(xnT[:].rearrange("p k d -> p (k d)"), X[:], ACT.Copy).then_inc(s_xnT, 1)
                if cur:
                    act.wait_ge(s_nb, i + 1)
                    at_least(act, s_rinv, i)
                    for s in range(NS):
                        nc.scalar.activation(probs[:, s, :], SC[:, s * S:(s + 1) * S], ACT.Exp,
                                             bias=nbias[:, s:s + 1], scale=SCALE,
                                             accum_out=rowsum[:, s:s + 1]).then_inc(s_exp, 1)
                if nxt:
                    act.wait_ge(s_CT, n + 1)
                    nc.scalar.activation(cT[:].rearrange("p k d -> p (k d)"), C[:], ACT.Copy).then_inc(s_cT, 1)
                if prev2:
                    act.wait_ge(s_gap, pp + 1)
                    nc.scalar.activation(egap[:], gap[:], ACT.Exp).then_inc(s_egap, 1)
                if nxt:
                    act.wait_ge(s_Q, n + 1)
                    for m in range(KD):
                        nc.scalar.activation(qT[:, m, :], Q[:, m * S:(m + 1) * S], ACT.Identity,
                                             bias=small[:, m:m + 1]).then_inc(s_qT, 1)
                if cur:
                    act.wait_ge(s_Z, i + 1)
                    nc.scalar.activation(zT[:].rearrange("p k d -> p (k d)"), Z[:], ACT.Copy).then_inc(s_zT, 1)
                if prev:
                    act.wait_ge(s_X2, p + 1)
                    nc.scalar.activation(x2T[:].rearrange("p k d -> p (k d)"), X[:], ACT.Copy).then_inc(s_x2T, 1)

            batches(act, step)

            def expert(j, c):
                b = 2 * j + c
                cur = not isinstance(b, int) or b < NBLK
                nxt = not isinstance(b, int) or b + 1 < NBLK
                if cur:
                    act.wait_ge(s_G, b + 1)
                    at_least(act, s_h, b)
                    nc.scalar.activation(sg[:], G[:], ACT.Silu).then_inc(s_silu, 1)
                if nxt:
                    act.wait_ge(s_XG, b + 2)
                    nc.scalar.activation(xgT[:].rearrange("p k d -> p (k d)"), XG[:, 0:D], ACT.Copy).then_inc(s_xgT, 1)
                if not isinstance(b, int) or b >= 1:
                    act.wait_ge(s_Y, b)
                    act.wait_ge(s_tabs[(c + 1) % 2], 16 * (j + (c - 1) // 2 + 1))
                    at_least(act, s_add, 16 * (b - 2))
                    q = (c + 1) % 2
                    nc.scalar.activation(y[:, q, :], Y[:, 0:D], ACT.Copy,
                                         scale=tab_s[:, q, 1:2].bitcast(F32)).then_inc(s_y, 1)

            act.wait_ge(s_XG, 1)
            nc.scalar.activation(xgT[:].rearrange("p k d -> p (k d)"), XG[:, 0:D], ACT.Copy).then_inc(s_xgT, 1)
            blocks(act, expert)

        @block.gpsimd
        def _(pool):
            g = nc.gpsimd
            g.memset(ident[:], 0.0).then_inc(s_const, 1)
            g.memset(before[:], 1.0).then_inc(s_const, 1)
            pool.wait_ge(s_const, 2)
            g.affine_select(out=ident[:], in_=ident[:], compare_op=ALU.not_equal, fill=1.0, base=0,
                            pattern=[[-1, P]], channel_multiplier=1).then_inc(s_const, 1)
            g.affine_select(out=before[:], in_=before[:], compare_op=ALU.is_gt, fill=0.0, base=0,
                            pattern=[[1, P]], channel_multiplier=-1).then_inc(s_const, 1)
            g.iota(spare[:, :, 0], [[1, P]], base=T, channel_multiplier=0).then_inc(s_spare, 1)
            g.memset(spare[:, :, 1], 0).then_inc(s_spare, 1)
            kw = dict(channel_multiplier=0, allow_small_or_imprecise_dtypes=True)
            g.iota(expert_no[:], [[0, NS], [0, TOP], [1, NE]], base=0, **kw).then_inc(s_const, 1)
            g.iota(expert_row[:], [[0, NS], [T, NE]], base=0, **kw).then_inc(s_const, 1)
            g.iota(block_edge[:], [[0, NE], [P, T // P]], base=0, **kw).then_inc(s_const, 1)
            g.iota(block_no[:], [[1, NMETA], [0, NE]], base=0, **kw).then_inc(s_const, 1)
            g.iota(entry[:, :, :, 0], [[P, NS], [0, TOP]], base=-S, channel_multiplier=1).then_inc(s_tok, 1)

            def rstd_of(which, s_in, s_eps, s_out, count):
                pool.wait_ge(s_in, count)
                own(pool, s_pool_here)
                g.tensor_scalar(var_eps[:, which, :], mv[:, which, :, 1], EPS, None, ALU.add).then_inc(s_eps, 1)
                pool.wait_ge(s_eps, count)
                g.tensor_tensor(rstd[:, which, :], var_eps[:, which, :], minus_half[:], ALU.pow).then_inc(s_out, 1)

            def turn(n):
                if isinstance(n, int):
                    pool.wait_ge(s_c0 if n == 0 else s_cr, 16)
                at_least(pool, s_CT, n)
                g.tensor_copy(c_turn[:], c_all[:, bass.ds(n, 1)].rearrange("p a s d -> p (a s) d")).then_inc(s_cturn, 1)

            pool.wait_ge(s_pre, 2)
            turn(0)
            rstd_of(0, s_st1, s_ve1, s_rs1, 1)

            def step(i):
                nxt, cur, prev, prev2 = part(i)
                n, p, pp = i + 1, i - 1, i - 2
                more = not isinstance(i, int) or i < B - 2
                if prev:
                    rstd_of(1, s_st2, s_ve2, s_rs2, p + 1)
                if cur:
                    if isinstance(i, int):
                        pool.wait_ge(s_x0 if i == 0 else s_xr, 16)
                        pool.wait_ge(s_folded, 5)
                    at_least(pool, s_x1, i)
                    for s in range(NS):
                        g.tensor_tensor(xb[:, s, :],
                                        x_all[:, bass.ds(i, 1), s].rearrange("p a d -> p (a d)"),
                                        bvo[:], ALU.add).then_inc(s_xb, 1)
                if more:
                    rstd_of(0, s_st1, s_ve1, s_rs1, i + 3)
                    turn(i + 2)
                if isinstance(i, int) and i == 1:
                    pool.wait_ge(s_filled, 32)
                if prev2:
                    pool.wait_ge(s_tok, 2 * pp + 2)
                    pool.wait_ge(s_slot, pp + 1)
                    pool.wait_ge(s_w1, pp + 1)
                    own(pool, s_pool_here)
                    for s in range(NS):
                        for k in range(TOP):
                            g.indirect_dma_start(
                                out=table[:, :], out_offset=bass.IndirectOffsetOnAxis(ap=slot[:, s, k:k + 1], axis=0),
                                in_=entry[:, s, k, :], in_offset=None).then_inc(s_scat, 16)
                if nxt:
                    at_least(pool, s_Z, n)
                    g.tensor_copy(c_val[:], c_all[:, bass.ds(n, 1)].rearrange("p a s d -> p (a s) d")).then_inc(s_cval, 1)

            batches(pool, step)

            def gather(j, c):
                q = c % 2
                pool.wait_ge(s_tabg[q], 16 * (j + c // 2 + 1))
                own(pool, s_pool_here)
                g.indirect_dma_start(
                    out=xg[:, q, :], out_offset=None, in_=xn_dram[:, :],
                    in_offset=bass.IndirectOffsetOnAxis(ap=tab_g[:, q, 0:1], axis=0)).then_inc(s_gath[q], 16)

            pool.wait_ge(s_store_xn, 16 * B)
            pool.wait_ge(s_store_x1, 16 * B)
            pool.wait_ge(s_zeroed, 32)
            gather(0, 0)
            gather(0, 1)

            def expert(j, c):
                b = 2 * j + c
                if not isinstance(b, int) or b + 2 < NBLK:
                    pool.wait_ge(s_XG, b + 1)
                    gather(j, c + 2)
                if not isinstance(b, int) or b >= 1:
                    q = (c + 1) % 2
                    pool.wait_ge(s_y, b)
                    at_least(pool, s_add, 16 * (b - 1))
                    own(pool, s_pool_here)
                    g.indirect_dma_start(
                        out=out[:, :], out_offset=bass.IndirectOffsetOnAxis(ap=tab_s[:, q, 0:1], axis=0),
                        in_=y[:, q, :], in_offset=None, compute_op=ALU.add).then_inc(s_add, 16)

            blocks(pool, expert)

        @block.vector
        def _(dve):
            v = nc.vector
            v.memset(zero_f[:], 0.0).then_inc(s_pre, 1)
            v.memset(ones_f[:], 1.0).then_inc(s_wide, 1)
            v.memset(ones_b[:], 1.0).then_inc(s_wide, 1)
            v.memset(so_far[:], 0.0).then_inc(s_acc, 1)
            v.memset(minus_half[:], -0.5).then_inc(s_pre, 1)

            def norm_stats(which, src, s_bn, s_out, count):
                for s in range(NS):
                    v.bn_stats(st[:, which, s, :], src(s)).then_inc(s_bn, 1)
                for s in range(NS):
                    dve.wait_ge(s_bn, NS * (count - 1) + s + 1)
                    own(dve, s_dve_here)
                    w = v.bn_aggr(mv[:, which, s, :], st[:, which, s, :])
                w.then_inc(s_out, 1)

            def x_of(b):
                return lambda s: x_all[:, bass.ds(b, 1), s].rearrange("p a d -> p (a d)")

            def norm_in(b):
                if isinstance(b, int):
                    dve.wait_ge(s_x0 if b == 0 else s_xr, 16)
                at_least(dve, s_xn, b)
                norm_stats(0, x_of(b), s_bn1, s_st1, b + 1)
                dve.wait_ge(s_rs1, b + 1)
                at_least(dve, s_XT, b)
                for s in range(NS):
                    w = v.tensor_scalar(xn[:, s, :], x_of(b)(s), mv[:, 0, s, 0:1], rstd[:, 0, s:s + 1],
                                        ALU.subtract, ALU.mult)
                w.then_inc(s_xn, 1)

            norm_in(0)
            dve.wait_ge(s_small, 80)
            dve.wait_ge(s_wide, 2)
            for k in range(KD):
                v.tensor_scalar(bq_wide[:, k, :], ones_f[:], bias_col[:, 0, k:k + 1], None, ALU.mult).then_inc(s_wide, 1)
                v.tensor_scalar(bv_wide[:, k, :], ones_f[:], bias_col[:, 2, k:k + 1], None, ALU.mult).then_inc(s_wide, 1)

            def step(i):
                nxt, cur, prev, prev2 = part(i)
                n, p, pp = i + 1, i - 1, i - 2
                if cur:
                    dve.wait_ge(s_S, i + 1)
                    at_least(dve, s_nb, i)
                    v.tensor_reduce(smax[:], SC[:].rearrange("p (s k) -> p s k", s=NS), AX_X, ALU.max).then_inc(s_max, 1)
                    dve.wait_ge(s_max, 3 * i + 1)
                    dve.wait_ge(s_qbk, i + 1)
                    v.tensor_tensor(full_max[:], smax[:], qbk[:], ALU.add).then_inc(s_max, 1)
                    dve.wait_ge(s_max, 3 * i + 2)
                    v.tensor_tensor(shift[:], qbk[:], full_max[:], ALU.subtract).then_inc(s_max, 1)
                    dve.wait_ge(s_max, 3 * i + 3)
                    v.tensor_scalar(nbias[:], shift[:], SCALE, None, ALU.mult).then_inc(s_nb, 1)
                if prev2:
                    dve.wait_ge(s_L, pp + 1)
                    at_least(dve, s_topi, NS * pp)
                    v.tensor_copy(logits[:].rearrange("p s e -> p (s e)"), M[:, 0:NS * NE]).then_inc(s_log, 1)
                    dve.wait_ge(s_log, pp + 1)
                    own(dve, s_dve_here)
                    for s in range(NS):
                        v.max(top_v[:, s, :], logits[:, s, :]).then_inc(s_topv, 1)
                    for s in range(NS):
                        dve.wait_ge(s_topv, NS * pp + s + 1)
                        own(dve, s_dve_here)
                        v.max_index(top_i[:, s, :], top_v[:, s, :], logits[:, s, :]).then_inc(s_topi, 1)
                    v.tensor_tensor(gap[:], top_v[:, :, 1], top_v[:, :, 0], ALU.subtract).then_inc(s_gap, 1)
                    dve.wait_ge(s_topi, NS * pp + NS)
                    v.tensor_copy(top_f[:], top_i[:, :, 0:TOP]).then_inc(s_topf, 1)
                    dve.wait_ge(s_topf, pp + 1)
                    v.tensor_tensor(onehot[:], expert_no[:], top_f[:].unsqueeze(3).to_broadcast([P, NS, TOP, NE]),
                                    ALU.is_equal).then_inc(s_hot, 1)
                    dve.wait_ge(s_hot, pp + 1)
                    at_least(dve, s_acc, NS * pp + 1)
                    v.tensor_tensor(member[:], onehot[:, :, 0, :], onehot[:, :, 1, :], ALU.add).then_inc(s_mem, 1)
                if prev:
                    dve.wait_ge(s_O, p + 1)
                    dve.wait_ge(s_xb, NS * (p + 1))
                    dve.wait_ge(s_rinv, p + 1)
                    at_least(dve, s_store_x1, 16 * p)
                    at_least(dve, s_xn2, p)
                    for s in range(NS):
                        w = v.scalar_tensor_tensor(out=x1[:, s, :], in0=O[:, s * D:(s + 1) * D], scalar=rinv[:, s:s + 1],
                                                   in1=xb[:, s, :], op0=ALU.mult, op1=ALU.add)
                    w.then_inc(s_x1, 1)
                    dve.wait_ge(s_x1, p + 1)
                    norm_stats(1, lambda s: x1[:, s, :], s_bn2, s_st2, p + 1)
                if nxt:
                    dve.wait_ge(s_QB, n + 1)
                    dve.wait_ge(s_folded, 3)
                    at_least(dve, s_max, 3 * n)
                    v.tensor_scalar(qbk[:], M[:, 32:32 + NS], small[:, 2 * KD:2 * KD + 1], None, ALU.add).then_inc(s_qbk, 1)
                if cur:
                    dve.wait_ge(s_PT, i + 1)
                    v.tensor_copy(pT[:].rearrange("p k d -> p (k d)"), PT[:]).then_inc(s_pT, 1)
                if prev:
                    dve.wait_ge(s_rs2, p + 1)
                    at_least(dve, s_store_xn, 16 * p)
                    for s in range(NS):
                        w = v.tensor_scalar(xn2[:, s, :], x1[:, s, :], mv[:, 1, s, 0:1], rstd[:, 1, s:s + 1],
                                            ALU.subtract, ALU.mult)
                    w.then_inc(s_xn2, 1)
                if cur:
                    dve.wait_ge(s_exp, NS * (i + 1))
                    at_least(dve, s_x1, i)
                    v.reciprocal(rinv[:], rowsum[:]).then_inc(s_rinv, 1)
                if not isinstance(i, int) or i < B - 2:
                    norm_in(i + 2)
                if prev2:
                    dve.wait_ge(s_POS, pp + 1)
                    v.tensor_tensor(pos[:].rearrange("p s e -> p (s e)"), M[:, 64:64 + NS * NE],
                                    expert_row[:].rearrange("p s e -> p (s e)"), ALU.add).then_inc(s_pos, 1)
                    dve.wait_ge(s_acc, NS * pp + 1)
                    for s in range(NS):
                        v.tensor_tensor(so_far[:], so_far[:], member[:, s, :], ALU.add).then_inc(s_acc, 1)
                        dve.wait_ge(s_acc, NS * pp + s + 2)
                    dve.wait_ge(s_pos, pp + 1)
                    for k in range(TOP):
                        w = v.tensor_tensor(picked[:, :, k, :], onehot[:, :, k, :], pos[:], ALU.mult)
                    w.then_inc(s_pick, 1)
                    dve.wait_ge(s_egap, pp + 1)
                    v.tensor_scalar(egap1[:], egap[:], 1.0, None, ALU.add).then_inc(s_eg1, 1)
                    dve.wait_ge(s_pick, pp + 1)
                    v.tensor_reduce(slot_f[:], picked[:], AX_X, ALU.add).then_inc(s_slotf, 1)
                    at_least(dve, s_scat, 16 * NS * TOP * pp)
                    dve.wait_ge(s_tok, 2 * pp + 1)
                    v.tensor_scalar(entry[:, :, :, 0], entry[:, :, :, 0], float(S), None, ALU.add).then_inc(s_tok, 2)
                    dve.wait_ge(s_slotf, pp + 1)
                    v.tensor_copy(slot[:], slot_f[:]).then_inc(s_slot, 1)
                    dve.wait_ge(s_eg1, pp + 1)
                    v.reciprocal(entry_f[:, :, 0, 1], egap1[:]).then_inc(s_w0, 1)
                    dve.wait_ge(s_w0, pp + 1)
                    v.tensor_tensor(entry_f[:, :, 1, 1], egap[:], entry_f[:, :, 0, 1], ALU.mult).then_inc(s_w1, 1)

            batches(dve, step)

            def link(ins, n):
                ins.then_inc(s_m, 1)
                dve.wait_ge(s_m, n)

            dve.wait_ge(s_CNT, 1)
            link(v.tensor_copy(cnt[:], M[:, 0:NE]), 1)
            link(v.tensor_tensor(over[:], cnt[:].unsqueeze(2).to_broadcast([P, NE, T // P]), block_edge[:], ALU.is_gt), 2)
            link(v.tensor_reduce(nblk[:], over[:], AX_X, ALU.add), 3)
            link(v.tensor_tensor_scan(ends[:], ones_f[:, 0:NE], nblk[:], 0.0, ALU.mult, ALU.add), 4)
            link(v.tensor_tensor(done[:], block_no[:], ends[:].unsqueeze(1).to_broadcast([P, NMETA, NE]), ALU.is_ge), 5)
            link(v.tensor_tensor(done_n[:], done[:], nblk[:].unsqueeze(1).to_broadcast([P, NMETA, NE]), ALU.mult), 6)
            link(v.tensor_reduce(blk_e[:], done[:], AX_X, ALU.add), 7)
            link(v.tensor_reduce(blk_s[:], done_n[:], AX_X, ALU.add), 8)
            link(v.tensor_tensor(blk_j[:], block_no[:, :, 0], blk_s[:], ALU.subtract), 9)
            link(v.tensor_scalar(blk_j[:], blk_j[:], float(P), None, ALU.mult), 10)
            link(v.scalar_tensor_tensor(out=blk_r[:], in0=blk_e[:], scalar=float(T), in1=blk_j[:],
                                        op0=ALU.mult, op1=ALU.add), 11)
            link(v.tensor_scalar(meta[:, 0, :], blk_e[:], float(NE - 1), None, ALU.min), 12)
            v.tensor_scalar(meta[:, 1, :], blk_r[:], float(ROWS), None, ALU.min).then_inc(s_meta, 1)

            def expert(j, c):
                b = 2 * j + c
                if not isinstance(b, int) or b < NBLK:
                    dve.wait_ge(s_silu, b + 1)
                    dve.wait_ge(s_U, b + 1)
                    at_least(dve, s_HT, b)
                    v.tensor_tensor(h[:], sg[:], U[:], ALU.mult).then_inc(s_h, 1)
                    dve.wait_ge(s_HT, b + 1)
                    v.tensor_copy(hT[:].rearrange("p k d -> p (k d)"), HT[:]).then_inc(s_hT, 1)

            blocks(dve, expert)

        @block.tensor
        def _(pe):
            t = nc.tensor

            def turned(dst, src, cols):
                for s in range(src.shape[1]):
                    for k in range(cols):
                        w = t.transpose(dst[:, k * src.shape[1] * P + s * P:k * src.shape[1] * P + (s + 1) * P],
                                        src[:, s, k * P:(k + 1) * P], ident[:])
                return w

            pe.wait_ge(s_const, 4)
            pe.wait_ge(s_wo, 16)
            turned(PT, wo_sb, KD).then_inc(s_fold, 1)
            pe.wait_ge(s_wq, 16)
            pe.wait_ge(s_wk, 16)
            for m in range(KD):
                for k in range(KD):
                    w = t.matmul(Z[:, m * D:(m + 1) * D], wq_sb[:, k, m * P:(m + 1) * P], wk_sb[:, k, :],
                                 start=(k == 0), stop=(k == KD - 1))
            w.then_inc(s_fold, 1)
            pe.wait_ge(s_small, 80)
            pe.wait_ge(s_wide, 6)
            for n, wt in ((0, wk_sb), (1, wq_sb)):
                for m in range(KD):
                    for k in range(KD):
                        t.matmul(M[:, n * KD + m:n * KD + m + 1], wt[:, k, m * P:(m + 1) * P],
                                 bias_col[:, n, k:k + 1], start=(k == 0), stop=(k == KD - 1))
            for k in range(KD):
                w = t.matmul(M[:, 2 * KD:2 * KD + 1], bq_wide[:, k, :], bias_col[:, 1, k:k + 1],
                             start=(k == 0), stop=(k == KD - 1))
            w.then_inc(s_fold, 1)
            pe.wait_ge(s_wv, 16)
            pe.wait_ge(s_folded, 1)
            for m in range(KD):
                for k in range(KD):
                    w = t.matmul(SC[:, m * D:(m + 1) * D], wv_sb[:, k, m * P:(m + 1) * P], woT[:, k, :],
                                 start=(k == 0), stop=(k == KD - 1))
            w.then_inc(s_fold, 1)
            for k in range(KD):
                t.matmul(O[:, 0:D], bv_wide[:, k, :], woT[:, k, :], start=(k == 0), stop=False)
            t.matmul(O[:, 0:D], ones_f[0:1, :], bo_row[0:1, :], start=False, stop=True).then_inc(s_fold, 1)
            pe.wait_ge(s_folded, 5)

            def step(i):
                nxt, cur, prev, prev2 = part(i)
                n, p, pp = i + 1, i - 1, i - 2
                if cur:
                    pe.wait_ge(s_qT, KD * (i + 1))
                    pe.wait_ge(s_cT, i + 1)
                    at_least(pe, s_exp, NS * i)
                    for s in range(NS):
                        for k in range(KD):
                            w = t.matmul(SC[:, s * S:(s + 1) * S], qT[:, k, s * P:(s + 1) * P], cT[:, k, :],
                                         start=(k == 0), stop=(k == KD - 1))
                    w.then_inc(s_S, 1)
                if nxt:
                    pe.wait_ge(s_xn, n + 1)
                    at_least(pe, s_x2T, i - 1)
                    turned(X, xn, KD).then_inc(s_XT, 1)
                    pe.wait_ge(s_cturn, n + 1)
                    turned(C, c_turn, KD).then_inc(s_CT, 1)
                if prev2:
                    pe.wait_ge(s_x2T, pp + 1)
                    at_least(pe, s_pos, pp)
                    if isinstance(i, int):
                        at_least(pe, s_qbk, min(n, B))
                    else:
                        pe.wait_ge(s_qbk, n)
                    for s in range(NS):
                        for k in range(KD):
                            w = t.matmul(M[:, s * NE:(s + 1) * NE], x2T[:, k, s * P:(s + 1) * P], router_sb[:, k, :],
                                         start=(k == 0), stop=(k == KD - 1))
                    w.then_inc(s_L, 1)
                if prev:
                    pe.wait_ge(s_zT, p + 1)
                    at_least(pe, s_x1, p)
                    for s in range(NS):
                        for k in range(KD):
                            w = t.matmul(O[:, s * D:(s + 1) * D], zT[:, k, s * P:(s + 1) * P], mvo[:, k, :],
                                         start=(k == 0), stop=(k == KD - 1))
                    w.then_inc(s_O, 1)

                def project(m):
                    for k in range(KD):
                        w = t.matmul(Q[:, m * S:(m + 1) * S], bT[:, k, m * P:(m + 1) * P], xnT[:, k, :],
                                     start=(k == 0), stop=(k == KD - 1))
                    return w

                if nxt:
                    pe.wait_ge(s_xnT, n + 1)
                    project(0)
                    if prev2:
                        pe.wait_ge(s_log, pp + 1)
                    for s in range(NS):
                        for k in range(KD):
                            w = t.matmul(M[:, 32 + s:33 + s], xnT[:, k, s * P:(s + 1) * P],
                                         small[:, KD + k:KD + k + 1], start=(k == 0), stop=(k == KD - 1))
                    w.then_inc(s_QB, 1)
                if cur:
                    pe.wait_ge(s_exp, NS * (i + 1))
                    at_least(pe, s_pT, i)
                    turned(PT, probs, NS).then_inc(s_PT, 1)
                if nxt:
                    project(1).then_inc(s_Q, 1)
                if prev2:
                    pe.wait_ge(s_mem, pp + 1)
                    if nxt:
                        pe.wait_ge(s_qbk, n + 1)
                    pe.wait_ge(s_acc, NS * pp + 1)
                    for s in range(NS):
                        o = M[:, 64 + s * NE:64 + (s + 1) * NE]
                        t.matmul(o, before[:], member[:, s, :], start=True, stop=False)
                        w = t.matmul(o, ones_b[:], so_far[:], start=False, stop=(s == 0))
                        if s == 1:
                            w = t.matmul(o, ones_b[:], member[:, 0, :], start=False, stop=True)
                    w.then_inc(s_POS, 1)
                if cur:
                    pe.wait_ge(s_pT, i + 1)
                    pe.wait_ge(s_cval, i + 1)
                    for m in range(KD):
                        for k in range(NS):
                            w = t.matmul(Z[:, m * S:(m + 1) * S], c_val[:, k, m * P:(m + 1) * P], pT[:, k, :],
                                         start=(k == 0), stop=(k == NS - 1))
                    w.then_inc(s_Z, 1)
                if prev:
                    pe.wait_ge(s_xn2, p + 1)
                    turned(X, xn2, KD).then_inc(s_X2, 1)

            batches(pe, step)

            pe.wait_ge(s_acc, NS * B + 1)
            t.matmul(M[:, 0:NE], ones_b[:], so_far[:], start=True, stop=True).then_inc(s_CNT, 1)

            def turn_tokens(j, c):
                pe.wait_ge(s_gath[c % 2], 16 * (j + c // 2 + 1))
                for k in range(KD):
                    w = t.transpose(XG[:, k * P:(k + 1) * P], xg[:, c % 2, k * P:(k + 1) * P], ident[:])
                w.then_inc(s_XG, 1)

            pe.wait_ge(s_meta, 1)
            turn_tokens(0, 0)
            pe.wait_ge(s_w13, 16 * NE)
            pe.wait_ge(s_w2, 16 * NE)

            def expert_of(j, c):
                return pe.value_load(meta[0:1, 0, bass.ds(2 * j + c, 1)], min_val=0, max_val=NE - 1)

            def expert(j, c):
                b = 2 * j + c
                if not isinstance(b, int) or b < NBLK:
                    e = expert_of(j, c)
                    pe.wait_ge(s_xgT, b + 1)
                    at_least(pe, s_silu, b)
                    for k in range(KD):
                        w = t.matmul(G[:], xgT[:, k, :], w13_sb[:, bass.ds(e * (KD * F2) + k * F2, F)],
                                     start=(k == 0), stop=(k == KD - 1))
                    w.then_inc(s_G, 1)
                    at_least(pe, s_h, b)
                    for k in range(KD):
                        w = t.matmul(U[:], xgT[:, k, :], w13_sb[:, bass.ds(e * (KD * F2) + k * F2 + F, F)],
                                     start=(k == 0), stop=(k == KD - 1))
                    w.then_inc(s_U, 1)
                if not isinstance(b, int) or b + 1 < NBLK:
                    turn_tokens(j, c + 1)
                if not isinstance(b, int) or b >= 1:
                    e = expert_of(j, c - 1)
                    pe.wait_ge(s_hT, b)
                    at_least(pe, s_y, b - 1)
                    for k in range(KF):
                        w = t.matmul(Y[:, 0:D], hT[:, k, :], w2_sb[:, bass.ds(e * (KF * D) + k * D, D)],
                                     start=(k == 0), stop=(k == KF - 1))
                    w.then_inc(s_Y, 1)
                if not isinstance(b, int) or b < NBLK:
                    pe.wait_ge(s_h, b + 1)
                    for k in range(KF):
                        w = t.transpose(HT[:, k * P:(k + 1) * P], h[:, k * P:(k + 1) * P], ident[:])
                    w.then_inc(s_HT, 1)

            blocks(pe, expert)


_INS = ["x", "ctx_1024", "L0_xattn_Wq", "L0_xattn_bq", "L0_xattn_Wk", "L0_xattn_bk", "L0_xattn_Wv", "L0_xattn_bv",
        "L0_xattn_Wo", "L0_xattn_bo", "L0_ffn_moe_router", "L0_ffn_moe_w13", "L0_ffn_moe_w2"]


def kernel(**inputs):
    import numpy as _np
    import concourse.bacc as _bacc
    from concourse import mybir as _mybir
    from concourse.bass_utils import run_bass_kernel_spmd as _run

    nc = _bacc.Bacc("TRN2", target_bir_lowering=False, num_devices=1)
    arrays, args = {}, []
    for name in _INS:
        a = _np.ascontiguousarray(inputs[name])
        arrays[f"in_{name}_dram"] = a
        args.append(nc.dram_tensor(f"in_{name}_dram", a.shape, _mybir.dt.from_np(a.dtype), kind="ExternalInput").ap())
    shape = inputs["x"].shape
    tokens = shape[0] * shape[1]
    args.append(nc.dram_tensor("out_0_dram", (tokens + 128, shape[2]), _mybir.dt.float32, kind="ExternalOutput").ap())
    xattn_moe(nc, *args)
    r = _run(nc, [arrays], core_ids=[0])
    return r.results[0]["out_0_dram"][:tokens].reshape(shape)
```

```python
from contextlib import ExitStack

import concourse.bass as bass
from concourse import mybir

F32 = mybir.dt.float32
F32R = mybir.dt.float32r
BF16 = mybir.dt.bfloat16
I32 = mybir.dt.int32
U32 = mybir.dt.uint32
ALU = mybir.AluOpType
ACT = mybir.ActivationFunctionType
AX_X = mybir.AxisListType.X

P = 128
EPS = 1e-5
TOP = 2


def at_least(engine, semaphore, count):
    if not (isinstance(count, int) and count <= 0):
        engine.wait_ge(semaphore, count)


def own(engine, semaphore):
    engine.sem_inc(semaphore, 1)


def xattn_moe(nc, x, ctx_in, wq, bq, wk, bk, wv, bv, wo, bo, router, w13, w2, out):
    B, S, D = x.shape
    NE, _, F2 = w13.shape
    F = F2 // 2
    T = B * S
    KD = D // P
    KF = F // P
    NS = S // P
    NBLK = (TOP * T + NE * (P - 1)) // P
    NMETA = NBLK + 1
    ROWS = NE * T
    SCALE = float(D) ** -0.5
    assert KD == 2 and NS == 2 and S == 256 and F == 512 and out.shape[0] == T + P

    xn_dram = nc.dram_tensor("xn_dram", (T + P, D), F32).ap()
    table = nc.dram_tensor("token_table", (ROWS + P, 2), I32).ap()

    with ExitStack() as ctx:
        def sb(name, shape, dt=F32):
            return ctx.enter_context(nc.sbuf_tensor(name, shape, dt))

        def bank(name):
            return ctx.enter_context(nc.psum_tensor(name, [P, 512], F32))

        def sem(name):
            return ctx.enter_context(nc.semaphore(name))

        w13_hi = sb("w13_hi", [P, NE * KD * F2], F32R)
        w13_lo = sb("w13_lo", [P, NE * KD * F2], F32R)
        w13_raw = sb("w13_raw", [P, F2])
        w2_sb = sb("w2_sb", [P, NE * KF * D])

        ident = sb("ident", [P, P])
        ones_f = sb("ones_f", [P, P])
        before = sb("before", [P, P], BF16)
        ones_b = sb("ones_b", [P, P], BF16)
        expert_no = sb("expert_no", [P, NS, TOP, NE])
        expert_row = sb("expert_row", [P, NS, NE])
        block_edge = sb("block_edge", [P, NE, T // P])
        block_no = sb("block_no", [P, NMETA, NE])
        minus_half = sb("minus_half", [P, NS])

        bT = sb("bT", [P, KD, D])
        mvo = sb("mvo", [P, KD, D])
        router_sb = sb("router_sb", [P, KD, NE])
        bias_col = sb("bias_col", [P, 3, KD])
        bo_row = sb("bo_row", [1, D])
        small = sb("small", [P, 2 * KD + 1])
        bvo = sb("bvo", [P, D])

        x_ln = sb("x_ln", [P, NS, D])
        x_res = sb("x_res", [P, NS, D])
        c_turn = sb("c_turn", [P, NS, D])
        c_val = sb("c_val", [P, NS, D])
        xn = sb("xn", [P, NS, D])
        xnT = sb("xnT", [P, KD, S])
        cT = sb("cT", [P, KD, S])
        qT = sb("qT", [P, KD, S])
        probs = sb("probs", [P, NS, S])
        pT = sb("pT", [P, NS, S])
        zT = sb("zT", [P, KD, S])
        x1 = sb("x1", [P, NS, D])
        xn2 = sb("xn2", [P, NS, D])
        x2T = sb("x2T", [P, KD, S])
        zero_f = x_res[:, 0, :]
        spare = x_res[:, 1, :].bitcast(I32).rearrange("p (c w) -> p c w", w=2)
        wq_sb, wk_sb, wv_sb, wo_sb, woT = probs, pT, zT, x1, xn2
        bq_wide, bv_wide = (x2T[:, n, :].rearrange("p (k c) -> p k c", k=KD) for n in range(2))
        st = sb("st", [P, 2, NS, 6])
        mv = sb("mv", [P, 2, NS, 2])
        rstd = sb("rstd", [P, 2, NS])
        var_eps = sb("var_eps", [P, 2, NS])
        smax = sb("smax", [P, NS])
        full_max = sb("full_max", [P, NS])
        nbias = sb("nbias", [P, NS])
        rowsum = sb("rowsum", [P, NS])
        rinv = sb("rinv", [P, NS])
        qbk = sb("qbk", [P, NS])

        logits = sb("logits", [P, NS, NE])
        top_v = sb("top_v", [P, NS, 8])
        top_i = sb("top_i", [P, NS, 8], U32)
        top_f = sb("top_f", [P, NS, TOP])
        onehot = sb("onehot", [P, NS, TOP, NE])
        member = sb("member", [P, NS, NE], BF16)
        so_far = sb("so_far", [P, NE], BF16)
        pos = sb("pos", [P, NS, NE])
        picked = sb("picked", [P, NS, TOP, NE])
        slot_f = sb("slot_f", [P, NS, TOP])
        slot = sb("slot", [P, 2, NS, TOP], I32)
        gap = sb("gap", [P, NS])
        egap = sb("egap", [P, NS])
        egap1 = sb("egap1", [P, NS])
        entry = sb("entry", [P, 2, NS, TOP, 2], I32)
        entry_f = entry[:].bitcast(F32)

        cnt = sb("cnt", [P, NE])
        over = xn[:, 0, 0:NE * (T // P)].rearrange("p (e n) -> p e n", e=NE)
        nblk = sb("nblk", [P, NE])
        ends = sb("ends", [P, NE])
        done, done_n = (z[:].rearrange("p k d -> p (k d)")[:, 0:NMETA * NE].rearrange("p (b e) -> p b e", b=NMETA)
                        for z in (cT, qT))
        blk_e = sb("blk_e", [P, NMETA])
        blk_s = sb("blk_s", [P, NMETA])
        blk_j = sb("blk_j", [P, NMETA])
        blk_r = sb("blk_r", [P, NMETA])
        meta = sb("meta", [P, 2, NMETA], I32)

        tab_g = sb("tab_g", [P, 2, 2], I32)
        tab_s = sb("tab_s", [P, 2, 2], I32)
        xgT_hi = sb("xgT_hi", [P, KD, P], F32R)
        xgT_lo = sb("xgT_lo", [P, KD, P], F32R)
        xg, y = c_turn, x_ln
        sg, h = (z[:].rearrange("p k d -> p (k d)") for z in (xnT, probs))
        hT = zT[:].rearrange("p k (j c) -> p (k j) c", c=P)

        banks = [bank(f"bank{n}") for n in range(8)]
        X, C, Q, SC, PT, Z, O, M = banks
        G, U, XG, HT, Y = banks[:5]

        s_wq, s_wk, s_wv, s_wo, s_small = (sem(f"s_{n}") for n in ("wq", "wk", "wv", "wo", "small"))
        s_xl, s_xs, s_raw, s_hi, s_lo = (sem(f"s_{n}") for n in ("xl", "xs", "raw", "hi", "lo"))
        s_dve_here, s_pool_here = sem("s_dve_here"), sem("s_pool_here")
        s_w2 = sem("s_w2")
        s_rooms = [sem("s_room_early"), sem("s_room_late")]
        s_zeroed, s_filled = sem("s_zeroed"), sem("s_filled")
        s_const, s_pre, s_wide, s_spare = (sem(f"s_{n}") for n in ("const", "pre", "wide", "spare"))
        s_fold, s_folded = sem("s_fold"), sem("s_folded")
        s_xn, s_xnT, s_XT, s_CT, s_cT, s_cturn, s_cval = (
            sem(f"s_{n}") for n in ("xn", "xnT", "XT", "CT", "cT", "cturn", "cval"))
        s_Q, s_qT, s_QB, s_qbk, s_S, s_max, s_nb, s_exp, s_rinv = (
            sem(f"s_{n}") for n in ("Q", "qT", "QB", "qbk", "S", "max", "nb", "exp", "rinv"))
        s_PT, s_pT, s_Z, s_zT, s_O, s_x1, s_xb = (
            sem(f"s_{n}") for n in ("PT", "pT", "Z", "zT", "O", "x1", "xb"))
        s_st1, s_ve1, s_rs1, s_st2, s_ve2, s_rs2, s_xn2, s_X2, s_x2T = (
            sem(f"s_{n}") for n in ("st1", "ve1", "rs1", "st2", "ve2", "rs2", "xn2", "X2", "x2T"))
        s_bn1, s_bn2 = sem("s_bn1"), sem("s_bn2")
        s_store_x1, s_store_xn = sem("s_store_x1"), sem("s_store_xn")
        s_L, s_log, s_topv, s_topi, s_topf, s_gap, s_egap, s_eg1, s_hot, s_mem, s_acc = (
            sem(f"s_{n}") for n in ("L", "log", "topv", "topi", "topf", "gap", "egap", "eg1", "hot", "mem", "acc"))
        s_POS, s_pos, s_pick, s_slotf, s_slot, s_w0, s_w1, s_tok = (
            sem(f"s_{n}") for n in ("POS", "pos", "pick", "slotf", "slot", "w0", "w1", "tok"))
        s_scat = [sem(f"s_scat{n}") for n in range(2)]
        s_CNT, s_m, s_meta = sem("s_CNT"), sem("s_m"), sem("s_meta")
        s_tabg = [sem(f"s_tabg{n}") for n in range(2)]
        s_tabs = [sem(f"s_tabs{n}") for n in range(2)]
        s_gath = [sem(f"s_gath{n}") for n in range(2)]
        s_XG, s_xgh, s_xgl, s_G, s_U, s_silu, s_h, s_HT, s_hT, s_Y, s_y, s_add = (
            sem(f"s_{n}") for n in ("XG", "xgh", "xgl", "G", "U", "silu", "h", "HT", "hT", "Y", "y", "add"))

        x_v = x.rearrange("b (s p) d -> b p s d", p=P)
        c_v = ctx_in.rearrange("b (s p) d -> b p s d", p=P)
        w13_v = w13.rearrange("e (k p) f -> (e k) p f", p=P)
        w2_v = w2.rearrange("e (k p) d -> e p k d", p=P)
        rows_v = out[0:T].rearrange("(b s p) d -> b p s d", p=P, s=NS)
        xn_v = xn_dram[0:T].rearrange("(b s p) d -> b p s d", p=P, s=NS)

        def part(i):
            if not isinstance(i, int):
                return True, True, True, True
            return -1 <= i < B - 1, 0 <= i < B, 1 <= i <= B, 2 <= i <= B + 1

        def batches(engine, step):
            for i in range(-1, 3):
                step(i)
            with engine.Fori(3, B - 2) as i:
                step(i)
            for i in range(B - 2, B + 2):
                step(i)

        def entry_of(pp):
            if not isinstance(pp, int) or pp < 4:
                return 0, pp, 1
            turn = pp - 4
            return (turn + 1) % 2, turn // 2 + (0 if turn % 2 == 0 else 4), (5 if pp == 4 else 2)

        EARLY, LATE = B + 4, B + 6
        rooms = {EARLY: (c_val, pT), LATE: (bT, xnT)}
        assert NE * KD == LATE + 2

        def at_end(i):
            return EARLY + 1 if isinstance(i, int) and i == B + 1 else i + 3

        def through_raw(n):
            return n - sum(n > m for m in rooms) if isinstance(n, int) else n

        def halves_of(n):
            if isinstance(n, int) and n in rooms:
                return [(room[:].rearrange("p a d -> p (a d)"), c * F, F) for c, room in enumerate(rooms[n])]
            return [(w13_raw[:], 0, F2)]

        def blocks(engine, step):
            for b in range(3):
                step(0, b)
            with engine.Fori(1, (NBLK - 3) // 2) as j:
                step(j, 1)
                step(j, 2)
            for b in range(NBLK - 2, NBLK + 1):
                step(0, b)

        assert NBLK % 2 == 1

        block = ctx.enter_context(nc.Block())

        @block.sync
        def _(sp):
            def kp(w):
                return w.rearrange("(k p) d -> p k d", p=P)

            def norm_operand(b):
                at_least(sp, s_xn, b)
                sp.dma_start(x_ln[:], x_v[b]).then_inc(s_xl, 16)

            def turn_operand(b):
                at_least(sp, s_CT, b)
                sp.dma_start(c_turn[:], c_v[b]).then_inc(s_cturn, 16)

            def raw(n):
                free = n - 1 if isinstance(n, int) and n - 1 in rooms else n
                at_least(sp, s_lo, free)
                sp.dma_start(w13_raw[:], w13_v[n]).then_inc(s_raw, 16)

            def raw_in_rooms(n, used, count):
                sp.wait_ge(used, count)
                for src, at, cols in halves_of(n):
                    sp.dma_start(src, w13_v[n][:, at:at + cols]).then_inc(s_rooms[n == LATE], 16)

            sp.dma_start(wq_sb[:], kp(wq)).then_inc(s_wq, 16)
            sp.dma_start(wk_sb[:], kp(wk)).then_inc(s_wk, 16)
            norm_operand(0)
            turn_operand(0)
            with nc.allow_non_contiguous_dma("three bias vectors turned into columns"):
                for n, b in enumerate((bq, bk, bv)):
                    sp.dma_start(bias_col[:, n, :], b.rearrange("(k p) -> p k", p=P)).then_inc(s_small, 16)
            sp.dma_start(bo_row[0:1, :], bo.rearrange("(a d) -> a d", a=1)).then_inc(s_small, 16)
            sp.dma_start(wo_sb[:], kp(wo)).then_inc(s_wo, 16)
            sp.dma_start(wv_sb[:], kp(wv)).then_inc(s_wv, 16)
            sp.dma_start(router_sb[:], kp(router)).then_inc(s_small, 16)
            raw(0)
            norm_operand(1)
            sp.wait_ge(s_pre, 1)
            sp.dma_start(xn_dram[T:T + P], zero_f).then_inc(s_zeroed, 16)
            sp.dma_start(out[T:T + P], zero_f).then_inc(s_zeroed, 16)
            sp.wait_ge(s_spare, 2)
            sp.dma_start(table[0:ROWS].rearrange("(p c) w -> p (c w)", p=P),
                         spare.rearrange("p c w -> p (c w)")).then_inc(s_filled, 16)
            sp.dma_start(table[ROWS:ROWS + P].rearrange("(a c) w -> a (c w)", a=1),
                         spare[0:1].rearrange("p c w -> p (c w)")).then_inc(s_filled, 16)
            turn_operand(1)
            raw(1)
            raw(2)

            def step(i):
                nxt, cur, prev, prev2 = part(i)
                p = i - 1
                more = not isinstance(i, int) or i < B - 2
                if more and cur:
                    norm_operand(i + 2)
                if cur:
                    at_least(sp, s_Z, i)
                    sp.dma_start(c_val[:], c_v[i]).then_inc(s_cval, 16)
                if more and cur:
                    turn_operand(i + 2)
                if not isinstance(i, int) or i >= 0:
                    raw(at_end(i))
                if isinstance(i, int) and i == B:
                    raw_in_rooms(EARLY, s_Z, B)
                    raw_in_rooms(LATE, s_Q, B)
                if cur:
                    sp.dma_start(w2_sb[:, bass.ds(i * (KF * D), KF * D)].rearrange("p (k d) -> p k d", k=KF),
                                 w2_v[i]).then_inc(s_w2, 16)
                if prev:
                    sp.wait_ge(s_x1, p + 1)
                    sp.dma_start(rows_v[p], x1[:]).then_inc(s_store_x1, 16)
                if cur:
                    if isinstance(i, int) and i == 0:
                        sp.wait_ge(s_zeroed, 32)
                        sp.wait_ge(s_filled, 32)
                    at_least(sp, s_x1, i)
                    sp.dma_start(x_res[:], x_v[i]).then_inc(s_xs, 16)
                if prev:
                    sp.wait_ge(s_xn2, p + 1)
                    sp.dma_start(xn_v[p], xn2[:]).then_inc(s_store_xn, 16)

            batches(sp, step)
            raw(LATE + 1)

            def first_row(j, c):
                return sp.value_load(meta[0:1, 1, bass.ds(2 * j + c, 1)], min_val=0, max_val=ROWS)

            def rows_gather(j, c):
                r = first_row(j, c)
                sp.dma_start(tab_g[:, c % 2, :], table[bass.ds(r, P), :]).then_inc(s_tabg[c % 2], 16)

            def rows_scatter(j, c):
                r = first_row(j, c)
                sp.dma_start(tab_s[:, c % 2, :], table[bass.ds(r, P), :]).then_inc(s_tabs[c % 2], 16)

            sp.wait_ge(s_meta, 1)
            for q in range(2):
                sp.wait_ge(s_scat[q], 16 * NS * TOP * (entry_of(B - 1 - q)[1] + 1))
            rows_gather(0, 0)
            rows_gather(0, 1)

            def load_rows(j, c):
                b = 2 * j + c
                if not isinstance(b, int) or b + 2 < NBLK:
                    sp.wait_ge(s_gath[c % 2], 16 * (j + c // 2 + 1))
                    rows_gather(j, c + 2)
                if not isinstance(b, int) or b < NBLK:
                    at_least(sp, s_add, 16 * (b - 1))
                    rows_scatter(j, c)

            blocks(sp, load_rows)
            sp.wait_ge(s_add, 16 * NBLK)
            sp.wait_ge(s_store_x1, 16 * B)
            sp.wait_ge(s_zeroed, 32)

        @block.scalar
        def _(act):
            def folded(count, dst, src):
                act.wait_ge(s_fold, count)
                nc.scalar.activation(dst, src, ACT.Copy).then_inc(s_folded, 1)

            def high(n):
                if isinstance(n, int) and n in rooms:
                    act.wait_ge(s_rooms[n == LATE], 32)
                else:
                    act.wait_ge(s_raw, 16 * (through_raw(n) + 1))
                for src, at, cols in halves_of(n):
                    w = nc.scalar.activation(w13_hi[:, bass.ds(n * F2 + at, cols)], src, ACT.Copy)
                w.then_inc(s_hi, 1)

            high(0)
            folded(1, bT[:].rearrange("p k d -> p (k d)"), Z[:])

            def step(i):
                nxt, cur, prev, prev2 = part(i)
                n, p, pp = i + 1, i - 1, i - 2
                if isinstance(i, int) and i == B + 1:
                    high(EARLY)
                if nxt:
                    act.wait_ge(s_XT, n + 1)
                    nc.scalar.activation(xnT[:].rearrange("p k d -> p (k d)"), X[:], ACT.Copy).then_inc(s_xnT, 1)
                if cur:
                    act.wait_ge(s_nb, i + 1)
                    at_least(act, s_rinv, i)
                    for s in range(NS):
                        nc.scalar.activation(probs[:, s, :], SC[:, s * S:(s + 1) * S], ACT.Exp,
                                             bias=nbias[:, s:s + 1], scale=SCALE,
                                             accum_out=rowsum[:, s:s + 1]).then_inc(s_exp, 1)
                if nxt:
                    act.wait_ge(s_CT, n + 1)
                    nc.scalar.activation(cT[:].rearrange("p k d -> p (k d)"), C[:], ACT.Copy).then_inc(s_cT, 1)
                if isinstance(i, int) and i == 0:
                    high(2)
                if isinstance(i, int) and i == -1:
                    folded(2, small[:], M[:, 0:2 * KD + 1])
                    folded(3, woT[:].rearrange("p k d -> p (k d)"), PT[:])
                    high(1)
                if prev2:
                    act.wait_ge(s_gap, pp + 1)
                    nc.scalar.activation(egap[:], gap[:], ACT.Exp).then_inc(s_egap, 1)
                if cur:
                    act.wait_ge(s_PT, i + 1)
                    at_least(act, s_Z, i)
                    nc.scalar.activation(pT[:].rearrange("p k d -> p (k d)"), PT[:], ACT.Copy).then_inc(s_pT, 1)
                if isinstance(i, int) and i == 0:
                    folded(5, bvo[:], O[:, 0:D])
                if nxt:
                    act.wait_ge(s_Q, n + 1)
                    for m in range(KD):
                        nc.scalar.activation(qT[:, m, :], Q[:, m * S:(m + 1) * S], ACT.Identity,
                                             bias=small[:, m:m + 1]).then_inc(s_qT, 1)
                if isinstance(i, int) and i == -1:
                    folded(4, mvo[:].rearrange("p k d -> p (k d)"), SC[:])
                if not isinstance(i, int) or i >= 0:
                    high(at_end(i))
                if cur:
                    act.wait_ge(s_Z, i + 1)
                    nc.scalar.activation(zT[:].rearrange("p k d -> p (k d)"), Z[:], ACT.Copy).then_inc(s_zT, 1)
                if prev:
                    act.wait_ge(s_X2, p + 1)
                    nc.scalar.activation(x2T[:].rearrange("p k d -> p (k d)"), X[:], ACT.Copy).then_inc(s_x2T, 1)

            batches(act, step)
            high(LATE)
            high(LATE + 1)

            def expert(j, c):
                b = 2 * j + c
                cur = not isinstance(b, int) or b < NBLK
                nxt = not isinstance(b, int) or b + 1 < NBLK
                if cur:
                    act.wait_ge(s_G, b + 1)
                    at_least(act, s_h, b)
                    nc.scalar.activation(sg, G[:], ACT.Silu).then_inc(s_silu, 1)
                if nxt:
                    act.wait_ge(s_XG, b + 2)
                    nc.scalar.activation(xgT_hi[:].rearrange("p k d -> p (k d)"), XG[:, 0:D], ACT.Copy).then_inc(s_xgh, 1)
                if not isinstance(b, int) or b >= 1:
                    act.wait_ge(s_Y, b)
                    act.wait_ge(s_tabs[(c + 1) % 2], 16 * (j + (c - 1) // 2 + 1))
                    at_least(act, s_add, 16 * (b - 2))
                    q = (c + 1) % 2
                    nc.scalar.activation(y[:, q, :], Y[:, 0:D], ACT.Copy,
                                         scale=tab_s[:, q, 1:2].bitcast(F32)).then_inc(s_y, 1)

            act.wait_ge(s_XG, 1)
            nc.scalar.activation(xgT_hi[:].rearrange("p k d -> p (k d)"), XG[:, 0:D], ACT.Copy).then_inc(s_xgh, 1)
            blocks(act, expert)

        @block.gpsimd
        def _(pool):
            g = nc.gpsimd
            g.memset(ident[:], 0.0).then_inc(s_const, 1)
            g.memset(before[:], 1.0).then_inc(s_const, 1)
            pool.wait_ge(s_const, 2)
            g.affine_select(out=ident[:], in_=ident[:], compare_op=ALU.not_equal, fill=1.0, base=0,
                            pattern=[[-1, P]], channel_multiplier=1).then_inc(s_const, 1)
            g.affine_select(out=before[:], in_=before[:], compare_op=ALU.is_gt, fill=0.0, base=0,
                            pattern=[[1, P]], channel_multiplier=-1).then_inc(s_const, 1)
            g.iota(spare[:, :, 0], [[1, P]], base=T, channel_multiplier=0).then_inc(s_spare, 1)
            g.memset(spare[:, :, 1], 0).then_inc(s_spare, 1)
            kw = dict(channel_multiplier=0, allow_small_or_imprecise_dtypes=True)
            g.iota(expert_no[:], [[0, NS], [0, TOP], [1, NE]], base=0, **kw).then_inc(s_const, 1)
            g.iota(expert_row[:], [[0, NS], [T, NE]], base=0, **kw).then_inc(s_const, 1)
            g.iota(block_edge[:], [[0, NE], [P, T // P]], base=0, **kw).then_inc(s_const, 1)
            g.iota(block_no[:], [[1, NMETA], [0, NE]], base=0, **kw).then_inc(s_const, 1)
            g.iota(entry[:, 0, :, :, 0], [[P, NS], [0, TOP]], base=-S, channel_multiplier=1).then_inc(s_tok, 1)
            g.iota(entry[:, 1, :, :, 0], [[P, NS], [0, TOP]], base=-S, channel_multiplier=1).then_inc(s_tok, 1)

            def rstd_of(which, s_in, s_eps, s_out, count):
                pool.wait_ge(s_in, count)
                own(pool, s_pool_here)
                g.tensor_scalar(var_eps[:, which, :], mv[:, which, :, 1], EPS, None, ALU.add).then_inc(s_eps, 1)
                pool.wait_ge(s_eps, count)
                g.tensor_tensor(rstd[:, which, :], var_eps[:, which, :], minus_half[:], ALU.pow).then_inc(s_out, 1)

            pool.wait_ge(s_pre, 2)
            rstd_of(0, s_st1, s_ve1, s_rs1, 1)

            def step(i):
                nxt, cur, prev, prev2 = part(i)
                n, p, pp = i + 1, i - 1, i - 2
                more = not isinstance(i, int) or i < B - 2
                if more:
                    rstd_of(0, s_st1, s_ve1, s_rs1, i + 3)
                if prev:
                    rstd_of(1, s_st2, s_ve2, s_rs2, p + 1)
                if cur:
                    pool.wait_ge(s_xs, 16 * (i + 1))
                    if isinstance(i, int):
                        pool.wait_ge(s_folded, 5)
                    for s in range(NS):
                        g.tensor_tensor(x_res[:, s, :], x_res[:, s, :], bvo[:], ALU.add).then_inc(s_xb, 1)
                if isinstance(i, int) and i == 1:
                    pool.wait_ge(s_filled, 32)
                if prev2:
                    q = entry_of(pp)[0]
                    pool.wait_ge(s_tok, 2 * pp + 3)
                    pool.wait_ge(s_slot, pp + 1)
                    pool.wait_ge(s_w1, pp + 1)
                    own(pool, s_pool_here)
                    for s in range(NS):
                        for k in range(TOP):
                            g.indirect_dma_start(
                                out=table[:, :], out_offset=bass.IndirectOffsetOnAxis(ap=slot[:, q, s, k:k + 1], axis=0),
                                in_=entry[:, q, s, k, :], in_offset=None).then_inc(s_scat[q], 16)

            batches(pool, step)

            def gather(j, c):
                q = c % 2
                pool.wait_ge(s_tabg[q], 16 * (j + c // 2 + 1))
                own(pool, s_pool_here)
                g.indirect_dma_start(
                    out=xg[:, q, :], out_offset=None, in_=xn_dram[:, :],
                    in_offset=bass.IndirectOffsetOnAxis(ap=tab_g[:, q, 0:1], axis=0)).then_inc(s_gath[q], 16)

            pool.wait_ge(s_store_xn, 16 * B)
            pool.wait_ge(s_store_x1, 16 * B)
            pool.wait_ge(s_zeroed, 32)
            gather(0, 0)
            gather(0, 1)

            def expert(j, c):
                b = 2 * j + c
                if not isinstance(b, int) or b + 2 < NBLK:
                    pool.wait_ge(s_XG, b + 1)
                    gather(j, c + 2)
                if not isinstance(b, int) or b >= 1:
                    q = (c + 1) % 2
                    pool.wait_ge(s_y, b)
                    at_least(pool, s_add, 16 * (b - 1))
                    own(pool, s_pool_here)
                    g.indirect_dma_start(
                        out=out[:, :], out_offset=bass.IndirectOffsetOnAxis(ap=tab_s[:, q, 0:1], axis=0),
                        in_=y[:, q, :], in_offset=None, compute_op=ALU.add).then_inc(s_add, 16)

            blocks(pool, expert)

        @block.vector
        def _(dve):
            v = nc.vector
            v.memset(zero_f, 0.0).then_inc(s_pre, 1)
            v.memset(ones_f[:], 1.0).then_inc(s_wide, 1)
            v.memset(ones_b[:], 1.0).then_inc(s_wide, 1)
            v.memset(so_far[:], 0.0).then_inc(s_acc, 1)
            v.memset(minus_half[:], -0.5).then_inc(s_pre, 1)

            def norm_stats(which, src, s_bn, s_out, count):
                for s in range(NS):
                    v.bn_stats(st[:, which, s, :], src(s)).then_inc(s_bn, 1)
                for s in range(NS):
                    dve.wait_ge(s_bn, NS * (count - 1) + s + 1)
                    own(dve, s_dve_here)
                    w = v.bn_aggr(mv[:, which, s, :], st[:, which, s, :])
                w.then_inc(s_out, 1)

            def norm_in_stats(b):
                dve.wait_ge(s_xl, 16 * (b + 1))
                at_least(dve, s_xn, b)
                norm_stats(0, lambda s: x_ln[:, s, :], s_bn1, s_st1, b + 1)

            def norm_in(b):
                dve.wait_ge(s_rs1, b + 1)
                at_least(dve, s_XT, b)
                for s in range(NS):
                    w = v.tensor_scalar(xn[:, s, :], x_ln[:, s, :], mv[:, 0, s, 0:1], rstd[:, 0, s:s + 1],
                                        ALU.subtract, ALU.mult)
                w.then_inc(s_xn, 1)

            norm_in_stats(0)
            norm_in(0)
            dve.wait_ge(s_small, 80)
            dve.wait_ge(s_wide, 2)
            for k in range(KD):
                v.tensor_scalar(bq_wide[:, k, :], ones_f[:], bias_col[:, 0, k:k + 1], None, ALU.mult).then_inc(s_wide, 1)
                v.tensor_scalar(bv_wide[:, k, :], ones_f[:], bias_col[:, 2, k:k + 1], None, ALU.mult).then_inc(s_wide, 1)

            def low(n):
                dve.wait_ge(s_hi, n + 1)
                for src, first, cols in halves_of(n):
                    at = bass.ds(n * F2 + first, cols)
                    w = v.tensor_tensor(w13_lo[:, at], src, w13_hi[:, at].bitcast(F32), ALU.subtract)
                w.then_inc(s_lo, 1)

            def rows(pp):
                dve.wait_ge(s_POS, pp + 1)
                v.tensor_tensor(pos[:].rearrange("p s e -> p (s e)"), M[:, 64:64 + NS * NE],
                                expert_row[:].rearrange("p s e -> p (s e)"), ALU.add).then_inc(s_pos, 1)
                dve.wait_ge(s_acc, NS * pp + 1)
                for s in range(NS):
                    v.tensor_tensor(so_far[:], so_far[:], member[:, s, :], ALU.add).then_inc(s_acc, 1)
                    dve.wait_ge(s_acc, NS * pp + s + 2)
                dve.wait_ge(s_pos, pp + 1)
                for k in range(TOP):
                    w = v.tensor_tensor(picked[:, :, k, :], onehot[:, :, k, :], pos[:], ALU.mult)
                w.then_inc(s_pick, 1)
                dve.wait_ge(s_egap, pp + 1)
                v.tensor_scalar(egap1[:], egap[:], 1.0, None, ALU.add).then_inc(s_eg1, 1)
                dve.wait_ge(s_pick, pp + 1)
                v.tensor_reduce(slot_f[:], picked[:], AX_X, ALU.add).then_inc(s_slotf, 1)
                q, before_this, back = entry_of(pp)
                at_least(dve, s_scat[q], 16 * NS * TOP * before_this)
                dve.wait_ge(s_tok, 2 * pp + 2)
                v.tensor_scalar(entry[:, q, :, :, 0], entry[:, q, :, :, 0], float(S * back), None,
                                ALU.add).then_inc(s_tok, 2)
                dve.wait_ge(s_slotf, pp + 1)
                v.tensor_copy(slot[:, q], slot_f[:]).then_inc(s_slot, 1)
                dve.wait_ge(s_eg1, pp + 1)
                v.reciprocal(entry_f[:, q, :, 0, 1], egap1[:]).then_inc(s_w0, 1)
                dve.wait_ge(s_w0, pp + 1)
                v.tensor_tensor(entry_f[:, q, :, 1, 1], egap[:], entry_f[:, q, :, 0, 1], ALU.mult).then_inc(s_w1, 1)

            low(0)

            def step(i):
                nxt, cur, prev, prev2 = part(i)
                n, p, pp = i + 1, i - 1, i - 2
                more = not isinstance(i, int) or i < B - 2
                if isinstance(i, int) and i == B + 1:
                    low(EARLY)
                if cur:
                    dve.wait_ge(s_S, i + 1)
                    at_least(dve, s_nb, i)
                    v.tensor_reduce(smax[:], SC[:].rearrange("p (s k) -> p s k", s=NS), AX_X, ALU.max).then_inc(s_max, 1)
                    dve.wait_ge(s_max, 2 * i + 1)
                    dve.wait_ge(s_qbk, i + 1)
                    v.scalar_tensor_tensor(out=full_max[:], in0=smax[:], scalar=SCALE, in1=qbk[:],
                                           op0=ALU.mult, op1=ALU.add).then_inc(s_max, 1)
                    dve.wait_ge(s_max, 2 * i + 2)
                    at_least(dve, s_exp, NS * i)
                    v.tensor_tensor(nbias[:], qbk[:], full_max[:], ALU.subtract).then_inc(s_nb, 1)
                if more:
                    norm_in_stats(i + 2)
                if isinstance(i, int) and i == 0:
                    low(2)
                if prev2:
                    dve.wait_ge(s_L, pp + 1)
                    at_least(dve, s_topi, NS * pp)
                    v.tensor_copy(logits[:].rearrange("p s e -> p (s e)"), M[:, 0:NS * NE]).then_inc(s_log, 1)
                    dve.wait_ge(s_log, pp + 1)
                    own(dve, s_dve_here)
                    for s in range(NS):
                        v.max(top_v[:, s, :], logits[:, s, :]).then_inc(s_topv, 1)
                    for s in range(NS):
                        dve.wait_ge(s_topv, NS * pp + s + 1)
                        own(dve, s_dve_here)
                        v.max_index(top_i[:, s, :], top_v[:, s, :], logits[:, s, :]).then_inc(s_topi, 1)
                    v.tensor_tensor(gap[:], top_v[:, :, 1], top_v[:, :, 0], ALU.subtract).then_inc(s_gap, 1)
                    dve.wait_ge(s_topi, NS * pp + NS)
                    v.tensor_copy(top_f[:], top_i[:, :, 0:TOP]).then_inc(s_topf, 1)
                    dve.wait_ge(s_topf, pp + 1)
                    v.tensor_tensor(onehot[:], expert_no[:], top_f[:].unsqueeze(3).to_broadcast([P, NS, TOP, NE]),
                                    ALU.is_equal).then_inc(s_hot, 1)
                    dve.wait_ge(s_hot, pp + 1)
                    at_least(dve, s_acc, NS * pp + 1)
                    v.tensor_tensor(member[:], onehot[:, :, 0, :], onehot[:, :, 1, :], ALU.add).then_inc(s_mem, 1)
                if prev:
                    dve.wait_ge(s_O, p + 1)
                    dve.wait_ge(s_xb, NS * (p + 1))
                    dve.wait_ge(s_rinv, p + 1)
                    at_least(dve, s_store_x1, 16 * p)
                    at_least(dve, s_xn2, p)
                    for s in range(NS):
                        w = v.scalar_tensor_tensor(out=x1[:, s, :], in0=O[:, s * D:(s + 1) * D], scalar=rinv[:, s:s + 1],
                                                   in1=x_res[:, s, :], op0=ALU.mult, op1=ALU.add)
                    w.then_inc(s_x1, 1)
                if nxt:
                    dve.wait_ge(s_QB, n + 1)
                    dve.wait_ge(s_folded, 2)
                    at_least(dve, s_nb, n)
                    v.tensor_scalar(qbk[:], M[:, 32:32 + NS], small[:, 2 * KD:2 * KD + 1], SCALE,
                                    ALU.add, ALU.mult).then_inc(s_qbk, 1)
                if prev:
                    dve.wait_ge(s_x1, p + 1)
                    norm_stats(1, lambda s: x1[:, s, :], s_bn2, s_st2, p + 1)
                if more:
                    norm_in(i + 2)
                if cur:
                    dve.wait_ge(s_exp, NS * (i + 1))
                    at_least(dve, s_x1, i)
                    v.reciprocal(rinv[:], rowsum[:]).then_inc(s_rinv, 1)
                tail = isinstance(i, int) and i == B
                if tail:
                    rows(pp)
                if prev:
                    dve.wait_ge(s_rs2, p + 1)
                    at_least(dve, s_store_xn, 16 * p)
                    for s in range(NS):
                        w = v.tensor_scalar(xn2[:, s, :], x1[:, s, :], mv[:, 1, s, 0:1], rstd[:, 1, s:s + 1],
                                            ALU.subtract, ALU.mult)
                    w.then_inc(s_xn2, 1)
                if prev2 and not tail:
                    rows(pp)
                if isinstance(i, int) and i == -1:
                    low(1)
                if not isinstance(i, int) or i >= 0:
                    low(at_end(i))

            batches(dve, step)

            def link(ins, n):
                ins.then_inc(s_m, 1)
                dve.wait_ge(s_m, n)

            dve.wait_ge(s_CNT, 1)
            link(v.tensor_copy(cnt[:], M[:, 0:NE]), 1)
            link(v.tensor_tensor(over, cnt[:].unsqueeze(2).to_broadcast([P, NE, T // P]), block_edge[:], ALU.is_gt), 2)
            link(v.tensor_reduce(nblk[:], over, AX_X, ALU.add), 3)
            link(v.tensor_tensor_scan(ends[:], ones_f[:, 0:NE], nblk[:], 0.0, ALU.mult, ALU.add), 4)
            link(v.tensor_tensor(done, block_no[:], ends[:].unsqueeze(1).to_broadcast([P, NMETA, NE]), ALU.is_ge), 5)
            link(v.tensor_tensor(done_n, done, nblk[:].unsqueeze(1).to_broadcast([P, NMETA, NE]), ALU.mult), 6)
            link(v.tensor_reduce(blk_e[:], done, AX_X, ALU.add), 7)
            link(v.tensor_reduce(blk_s[:], done_n, AX_X, ALU.add), 8)
            link(v.tensor_tensor(blk_j[:], block_no[:, :, 0], blk_s[:], ALU.subtract), 9)
            link(v.tensor_scalar(blk_j[:], blk_j[:], float(P), None, ALU.mult), 10)
            link(v.scalar_tensor_tensor(out=blk_r[:], in0=blk_e[:], scalar=float(T), in1=blk_j[:],
                                        op0=ALU.mult, op1=ALU.add), 11)
            link(v.tensor_scalar(meta[:, 0, :], blk_e[:], float(NE - 1), None, ALU.min), 12)
            v.tensor_scalar(meta[:, 1, :], blk_r[:], float(ROWS), None, ALU.min).then_inc(s_meta, 1)
            low(LATE)
            low(LATE + 1)

            def tokens_low(b):
                dve.wait_ge(s_xgh, b + 1)
                v.tensor_tensor(xgT_lo[:].rearrange("p k d -> p (k d)"), XG[:, 0:D],
                                xgT_hi[:].rearrange("p k d -> p (k d)").bitcast(F32), ALU.subtract).then_inc(s_xgl, 1)

            tokens_low(0)

            def expert(j, c):
                b = 2 * j + c
                if not isinstance(b, int) or b < NBLK:
                    dve.wait_ge(s_silu, b + 1)
                    dve.wait_ge(s_U, b + 1)
                    at_least(dve, s_HT, b)
                    v.tensor_tensor(h, sg, U[:], ALU.mult).then_inc(s_h, 1)
                    if not isinstance(b, int) or b + 1 < NBLK:
                        tokens_low(b + 1)
                    dve.wait_ge(s_HT, b + 1)
                    v.tensor_copy(zT[:].rearrange("p k d -> p (k d)"), HT[:]).then_inc(s_hT, 1)

            blocks(dve, expert)

        @block.tensor
        def _(pe):
            t = nc.tensor

            def turned(dst, src, cols):
                for s in range(src.shape[1]):
                    for k in range(cols):
                        w = t.transpose(dst[:, k * src.shape[1] * P + s * P:k * src.shape[1] * P + (s + 1) * P],
                                        src[:, s, k * P:(k + 1) * P], ident[:])
                return w

            def fold_biases():
                pe.wait_ge(s_small, 80)
                pe.wait_ge(s_wide, 6)
                for n, wt in ((0, wk_sb), (1, wq_sb)):
                    for m in range(KD):
                        for k in range(KD):
                            t.matmul(M[:, n * KD + m:n * KD + m + 1], wt[:, k, m * P:(m + 1) * P],
                                     bias_col[:, n, k:k + 1], start=(k == 0), stop=(k == KD - 1))
                for k in range(KD):
                    w = t.matmul(M[:, 2 * KD:2 * KD + 1], bq_wide[:, k, :], bias_col[:, 1, k:k + 1],
                                 start=(k == 0), stop=(k == KD - 1))
                w.then_inc(s_fold, 1)

            def turn_wo():
                pe.wait_ge(s_const, 4)
                pe.wait_ge(s_wo, 16)
                turned(PT, wo_sb, KD).then_inc(s_fold, 1)

            def fold_values():
                pe.wait_ge(s_wv, 16)
                pe.wait_ge(s_folded, 3)
                for m in range(KD):
                    for k in range(KD):
                        w = t.matmul(SC[:, m * D:(m + 1) * D], wv_sb[:, k, m * P:(m + 1) * P], woT[:, k, :],
                                     start=(k == 0), stop=(k == KD - 1))
                w.then_inc(s_fold, 1)

            def fold_value_bias():
                for k in range(KD):
                    t.matmul(O[:, 0:D], bv_wide[:, k, :], woT[:, k, :], start=(k == 0), stop=False)
                t.matmul(O[:, 0:D], ones_f[0:1, :], bo_row[0:1, :], start=False, stop=True).then_inc(s_fold, 1)

            pe.wait_ge(s_const, 4)
            pe.wait_ge(s_wq, 16)
            pe.wait_ge(s_wk, 16)
            for m in range(KD):
                for k in range(KD):
                    w = t.matmul(Z[:, m * D:(m + 1) * D], wq_sb[:, k, m * P:(m + 1) * P], wk_sb[:, k, :],
                                 start=(k == 0), stop=(k == KD - 1))
            w.then_inc(s_fold, 1)
            def step(i):
                nxt, cur, prev, prev2 = part(i)
                n, p, pp = i + 1, i - 1, i - 2
                if cur:
                    if isinstance(i, int) and i == 0:
                        pe.wait_ge(s_folded, 4)
                    pe.wait_ge(s_qT, KD * (i + 1))
                    pe.wait_ge(s_cT, i + 1)
                    at_least(pe, s_exp, NS * i)
                    for s in range(NS):
                        for k in range(KD):
                            w = t.matmul(SC[:, s * S:(s + 1) * S], qT[:, k, s * P:(s + 1) * P], cT[:, k, :],
                                         start=(k == 0), stop=(k == KD - 1))
                    w.then_inc(s_S, 1)
                if nxt:
                    pe.wait_ge(s_xn, n + 1)
                    at_least(pe, s_x2T, i - 1)
                    turned(X, xn, KD).then_inc(s_XT, 1)
                    pe.wait_ge(s_cturn, 16 * (n + 1))
                    turned(C, c_turn, KD).then_inc(s_CT, 1)
                if isinstance(i, int) and i == -1:
                    fold_biases()
                    turn_wo()
                if prev2:
                    pe.wait_ge(s_x2T, pp + 1)
                    at_least(pe, s_pos, pp)
                    if isinstance(i, int):
                        at_least(pe, s_qbk, min(n, B))
                    else:
                        pe.wait_ge(s_qbk, n)
                    for s in range(NS):
                        for k in range(KD):
                            w = t.matmul(M[:, s * NE:(s + 1) * NE], x2T[:, k, s * P:(s + 1) * P], router_sb[:, k, :],
                                         start=(k == 0), stop=(k == KD - 1))
                    w.then_inc(s_L, 1)
                if prev:
                    if isinstance(i, int) and i == 1:
                        pe.wait_ge(s_folded, 5)
                    pe.wait_ge(s_zT, p + 1)
                    at_least(pe, s_x1, p)
                    for s in range(NS):
                        for k in range(KD):
                            w = t.matmul(O[:, s * D:(s + 1) * D], zT[:, k, s * P:(s + 1) * P], mvo[:, k, :],
                                         start=(k == 0), stop=(k == KD - 1))
                    w.then_inc(s_O, 1)

                def project(m):
                    for k in range(KD):
                        w = t.matmul(Q[:, m * S:(m + 1) * S], bT[:, k, m * P:(m + 1) * P], xnT[:, k, :],
                                     start=(k == 0), stop=(k == KD - 1))
                    return w

                if nxt:
                    if isinstance(i, int) and i == -1:
                        pe.wait_ge(s_folded, 2)
                    pe.wait_ge(s_xnT, n + 1)
                    project(0)
                    if prev2:
                        pe.wait_ge(s_log, pp + 1)
                    for s in range(NS):
                        for k in range(KD):
                            w = t.matmul(M[:, 32 + s:33 + s], xnT[:, k, s * P:(s + 1) * P],
                                         small[:, KD + k:KD + k + 1], start=(k == 0), stop=(k == KD - 1))
                    w.then_inc(s_QB, 1)
                if cur:
                    pe.wait_ge(s_exp, NS * (i + 1))
                    at_least(pe, s_pT, i)
                    turned(PT, probs, NS).then_inc(s_PT, 1)
                if nxt:
                    project(1).then_inc(s_Q, 1)
                if isinstance(i, int) and i == -1:
                    fold_values()
                if isinstance(i, int) and i == 0:
                    fold_value_bias()
                if prev2:
                    pe.wait_ge(s_mem, pp + 1)
                    if nxt:
                        pe.wait_ge(s_qbk, n + 1)
                    pe.wait_ge(s_acc, NS * pp + 1)
                    for s in range(NS):
                        o = M[:, 64 + s * NE:64 + (s + 1) * NE]
                        t.matmul(o, before[:], member[:, s, :], start=True, stop=False)
                        w = t.matmul(o, ones_b[:], so_far[:], start=False, stop=(s == 0))
                        if s == 1:
                            w = t.matmul(o, ones_b[:], member[:, 0, :], start=False, stop=True)
                    w.then_inc(s_POS, 1)
                if cur:
                    pe.wait_ge(s_pT, i + 1)
                    pe.wait_ge(s_cval, 16 * (i + 1))
                    for m in range(KD):
                        for k in range(NS):
                            w = t.matmul(Z[:, m * S:(m + 1) * S], c_val[:, k, m * P:(m + 1) * P], pT[:, k, :],
                                         start=(k == 0), stop=(k == NS - 1))
                    w.then_inc(s_Z, 1)
                if prev:
                    pe.wait_ge(s_xn2, p + 1)
                    turned(X, xn2, KD).then_inc(s_X2, 1)

            batches(pe, step)

            pe.wait_ge(s_acc, NS * B + 1)
            t.matmul(M[:, 0:NE], ones_b[:], so_far[:], start=True, stop=True).then_inc(s_CNT, 1)

            def turn_tokens(j, c):
                pe.wait_ge(s_gath[c % 2], 16 * (j + c // 2 + 1))
                for k in range(KD):
                    w = t.transpose(XG[:, k * P:(k + 1) * P], xg[:, c % 2, k * P:(k + 1) * P], ident[:])
                w.then_inc(s_XG, 1)

            pe.wait_ge(s_meta, 1)
            turn_tokens(0, 0)
            pe.wait_ge(s_lo, NE * KD)
            pe.wait_ge(s_w2, 16 * NE)

            def expert_of(j, c):
                return pe.value_load(meta[0:1, 0, bass.ds(2 * j + c, 1)], min_val=0, max_val=NE - 1)

            def up(dst, e, column):
                first = True
                for x_part, w_part in ((xgT_hi, w13_hi), (xgT_hi, w13_lo), (xgT_lo, w13_hi)):
                    for k in range(KD):
                        w = t.matmul(dst[:], x_part[:, k, :], w_part[:, bass.ds(e * (KD * F2) + (k * F2 + column), F)],
                                     start=first, stop=(x_part is xgT_lo and k == KD - 1))
                        first = False
                return w

            def expert(j, c):
                b = 2 * j + c
                if not isinstance(b, int) or b < NBLK:
                    e = expert_of(j, c)
                    pe.wait_ge(s_xgl, b + 1)
                    at_least(pe, s_silu, b)
                    up(G, e, 0).then_inc(s_G, 1)
                    at_least(pe, s_h, b)
                    up(U, e, F).then_inc(s_U, 1)
                if not isinstance(b, int) or b + 1 < NBLK:
                    turn_tokens(j, c + 1)
                if not isinstance(b, int) or b >= 1:
                    e = expert_of(j, c - 1)
                    pe.wait_ge(s_hT, b)
                    at_least(pe, s_y, b - 1)
                    for k in range(KF):
                        w = t.matmul(Y[:, 0:D], hT[:, k, :], w2_sb[:, bass.ds(e * (KF * D) + k * D, D)],
                                     start=(k == 0), stop=(k == KF - 1))
                    w.then_inc(s_Y, 1)
                if not isinstance(b, int) or b < NBLK:
                    pe.wait_ge(s_h, b + 1)
                    for k in range(KF):
                        w = t.transpose(HT[:, k * P:(k + 1) * P], h[:, k * P:(k + 1) * P], ident[:])
                    w.then_inc(s_HT, 1)

            blocks(pe, expert)


_INS = ["x", "ctx_1024", "L0_xattn_Wq", "L0_xattn_bq", "L0_xattn_Wk", "L0_xattn_bk", "L0_xattn_Wv", "L0_xattn_bv",
        "L0_xattn_Wo", "L0_xattn_bo", "L0_ffn_moe_router", "L0_ffn_moe_w13", "L0_ffn_moe_w2"]


def kernel(**inputs):
    import numpy as _np
    import concourse.bacc as _bacc
    from concourse import mybir as _mybir
    from concourse.bass_utils import run_bass_kernel_spmd as _run

    nc = _bacc.Bacc("TRN2", target_bir_lowering=False, num_devices=1)
    arrays, args = {}, []
    for name in _INS:
        a = _np.ascontiguousarray(inputs[name])
        arrays[f"in_{name}_dram"] = a
        args.append(nc.dram_tensor(f"in_{name}_dram", a.shape, _mybir.dt.from_np(a.dtype), kind="ExternalInput").ap())
    shape = inputs["x"].shape
    tokens = shape[0] * shape[1]
    args.append(nc.dram_tensor("out_0_dram", (tokens + 128, shape[2]), _mybir.dt.float32, kind="ExternalOutput").ap())
    xattn_moe(nc, *args)
    r = _run(nc, [arrays], core_ids=[0])
    return r.results[0]["out_0_dram"][:tokens].reshape(shape)
```

```python
from contextlib import ExitStack

import concourse.bass as bass
from concourse import mybir

F32 = mybir.dt.float32
F32R = mybir.dt.float32r
BF16 = mybir.dt.bfloat16
I32 = mybir.dt.int32
U32 = mybir.dt.uint32
ALU = mybir.AluOpType
ACT = mybir.ActivationFunctionType
AX_X = mybir.AxisListType.X

P = 128
EPS = 1e-5
TOP = 2


def at_least(engine, semaphore, count):
    if not (isinstance(count, int) and count <= 0):
        engine.wait_ge(semaphore, count)


def own(engine, semaphore):
    engine.sem_inc(semaphore, 1)


def xattn_moe(nc, x, ctx_in, wq, bq, wk, bk, wv, bv, wo, bo, router, w13, w2, out):
    B, S, D = x.shape
    NE, _, F2 = w13.shape
    F = F2 // 2
    T = B * S
    KD = D // P
    KF = F // P
    NS = S // P
    NBLK = (TOP * T + NE * (P - 1)) // P
    NMETA = NBLK + 1
    ROWS = NE * T
    SCALE = float(D) ** -0.5
    assert KD == 2 and NS == 2 and S == 256 and F == 512 and out.shape[0] == T + P

    xn_dram = nc.dram_tensor("xn_dram", (T + P, D), F32).ap()
    table = nc.dram_tensor("token_table", (ROWS + P, 2), I32).ap()

    with ExitStack() as ctx:
        first = ExitStack()
        stage = ctx

        def sb(name, shape, dt=F32):
            return stage.enter_context(nc.sbuf_tensor(name, shape, dt))

        def bank(name):
            return ctx.enter_context(nc.psum_tensor(name, [P, 512], F32))

        def sem(name):
            return ctx.enter_context(nc.semaphore(name))

        w13_hi = sb("w13_hi", [P, NE * KD * F2], F32R)
        w13_lo = sb("w13_lo", [P, NE * KD * F2], F32R)
        ident = sb("ident", [P, P])
        meta = sb("meta", [P, 2, NMETA], I32)
        tab_g = sb("tab_g", [P, 2, 2], I32)
        tab_s = sb("tab_s", [P, 2, 2], I32)
        xgT_hi = sb("xgT_hi", [P, KD, P], F32R)
        xgT_lo = sb("xgT_lo", [P, KD, P], F32R)

        stage = first
        w2_raw = sb("w2_raw", [P, NE * KF * D])
        probs = sb("probs", [P, NS, S])
        xn = sb("xn", [P, NS, D])
        x_res = sb("x_res", [P, NS, D])
        zT = sb("zT", [P, KD, S])
        mvo = sb("mvo", [P, KD, D])
        bvo = sb("bvo", [P, D])
        wbk = sb("wbk", [P, D])
        x1 = sb("x1", [P, NS, D])
        xn2 = sb("xn2", [P, NS, D])
        x_ln = sb("x_ln", [P, NS, D])
        c_turn = sb("c_turn", [P, NS, D])
        bT = sb("bT", [P, KD, D])
        xnT = sb("xnT", [P, KD, S])
        qT = sb("qT", [P, KD, S])
        cT = sb("cT", [P, KD, S])
        c_val = sb("c_val", [P, NS, D])
        pT = sb("pT", [P, NS, S])
        x2T = sb("x2T", [P, KD, S])
        router_sb = sb("router_sb", [P, KD, NE])
        bias_col = sb("bias_col", [P, 3, KD])
        small = sb("small", [P, KD + 1])
        prod = sb("prod", [P, NS, D])
        qsum = sb("qsum", [P, NS])
        nmr = sb("nmr", [P, 2, NS])

        ones_f = sb("ones_f", [P, P])
        before = sb("before", [P, P], BF16)
        ones_b = sb("ones_b", [P, P], BF16)
        expert_no = sb("expert_no", [P, NS, TOP, NE])
        expert_row = sb("expert_row", [P, NS, NE])
        block_edge = sb("block_edge", [P, NE, T // P])
        block_no = sb("block_no", [P, NMETA, NE])
        minus_half = sb("minus_half", [P, NS])

        zero_f = x_res[:, 0, :]
        spare = x_res[:, 1, :].bitcast(I32).rearrange("p (c w) -> p c w", w=2)
        wq_sb, wk_sb, wv_sb, wo_sb, woT = probs, pT, zT, x1, xn2
        bk_wide, bv_wide = (x2T[:, n, :].rearrange("p (k c) -> p k c", k=KD) for n in range(2))
        bo_row = bvo[0:1, :]
        st = sb("st", [P, 2, NS, 6])
        mv = sb("mv", [P, 2, NS, 2])
        rstd = sb("rstd", [P, 2, NS])
        var_eps = sb("var_eps", [P, 2, NS])
        smax = sb("smax", [P, NS])
        full_max = sb("full_max", [P, NS])
        nbias = sb("nbias", [P, NS])
        rowsum = sb("rowsum", [P, NS])
        rinv = sb("rinv", [P, NS])
        qbk = sb("qbk", [P, NS])

        logits = sb("logits", [P, NS, NE])
        top_v = sb("top_v", [P, NS, 8])
        top_i = sb("top_i", [P, NS, 8], U32)
        top_f = sb("top_f", [P, NS, TOP])
        onehot = sb("onehot", [P, NS, TOP, NE])
        member = sb("member", [P, NS, NE], BF16)
        so_far = sb("so_far", [P, NE], BF16)
        pos = sb("pos", [P, NS, NE])
        picked = sb("picked", [P, NS, TOP, NE])
        slot_f = sb("slot_f", [P, NS, TOP])
        slot = sb("slot", [P, 2, NS, TOP], I32)
        gap = sb("gap", [P, NS])
        egap = sb("egap", [P, NS])
        egap1 = sb("egap1", [P, NS])
        entry = sb("entry", [P, 2, NS, TOP, 2], I32)
        entry_f = entry[:].bitcast(F32)

        cnt = sb("cnt", [P, NE])
        nblk = sb("nblk", [P, NE])
        ends = sb("ends", [P, NE])
        blk_e = sb("blk_e", [P, NMETA])
        blk_s = sb("blk_s", [P, NMETA])
        blk_r = sb("blk_r", [P, NMETA])
        room = x2T[:].rearrange("p k d -> p (k d)")
        done = room[:, 0:NMETA * NE].rearrange("p (b e) -> p b e", b=NMETA)
        over = room[:, NMETA * NE:NMETA * NE + NE * (T // P)].rearrange("p (e n) -> p e n", e=NE)
        w13_raw = sb("w13_raw", [P, F2])
        first.close()

        stage = ctx
        w2_lo = sb("w2_lo", [P, NE * KF * D], F32R)
        w2_hi = sb("w2_hi", [P, NE * KF * D], F32R)
        xg = sb("xg", [P, 2, D])
        y = sb("y", [P, 2, D])
        h = sb("h", [P, F])
        hT_hi = sb("hT_hi", [P, KF, P], F32R)
        hT_lo = sb("hT_lo", [P, KF, P], F32R)

        banks = [bank(f"bank{n}") for n in range(8)]
        X, C, Q, SC, PT, Z, O, M = banks
        G, U, XG, HT, Y = banks[:5]

        s_wq, s_wk, s_wv, s_wo, s_small = (sem(f"s_{n}") for n in ("wq", "wk", "wv", "wo", "small"))
        s_xl, s_xs, s_raw, s_hi, s_lo = (sem(f"s_{n}") for n in ("xl", "xs", "raw", "hi", "lo"))
        s_dve_here, s_pool_here, s_sp_here = sem("s_dve_here"), sem("s_pool_here"), sem("s_sp_here")
        s_small_out, s_prod, s_qsum, s_nmr1, s_nmr2 = (sem(f"s_{n}") for n in ("small_out", "prod", "qsum", "nmr1", "nmr2"))
        s_w2, s_w2hi, s_w2lo = sem("s_w2"), sem("s_w2hi"), sem("s_w2lo")
        s_rooms = [sem(f"s_room{n}") for n in range(6)]
        s_zeroed, s_filled = sem("s_zeroed"), sem("s_filled")
        s_const, s_pre, s_wide, s_spare = (sem(f"s_{n}") for n in ("const", "pre", "wide", "spare"))
        s_fold, s_folded = sem("s_fold"), sem("s_folded")
        s_xn, s_xnT, s_XT, s_CT, s_cT, s_cturn, s_cval = (
            sem(f"s_{n}") for n in ("xn", "xnT", "XT", "CT", "cT", "cturn", "cval"))
        s_Q, s_qT, s_qbk, s_S, s_max, s_nb, s_exp, s_rinv = (
            sem(f"s_{n}") for n in ("Q", "qT", "qbk", "S", "max", "nb", "exp", "rinv"))
        s_PT, s_pT, s_Z, s_zT, s_O, s_x1, s_xb = (
            sem(f"s_{n}") for n in ("PT", "pT", "Z", "zT", "O", "x1", "xb"))
        s_st1, s_ve1, s_rs1, s_st2, s_ve2, s_rs2, s_xn2, s_X2, s_x2T = (
            sem(f"s_{n}") for n in ("st1", "ve1", "rs1", "st2", "ve2", "rs2", "xn2", "X2", "x2T"))
        s_bn1, s_bn2 = sem("s_bn1"), sem("s_bn2")
        s_store_x1, s_store_xn = sem("s_store_x1"), sem("s_store_xn")
        s_L, s_log, s_topv, s_topi, s_topf, s_gap, s_egap, s_eg1, s_hot, s_mem, s_acc = (
            sem(f"s_{n}") for n in ("L", "log", "topv", "topi", "topf", "gap", "egap", "eg1", "hot", "mem", "acc"))
        s_POS, s_pos, s_pick, s_slotf, s_slot, s_w0, s_w1, s_tok = (
            sem(f"s_{n}") for n in ("POS", "pos", "pick", "slotf", "slot", "w0", "w1", "tok"))
        s_scat = [sem(f"s_scat{n}") for n in range(2)]
        s_CNT, s_m, s_meta = sem("s_CNT"), sem("s_m"), sem("s_meta")
        s_tabg = [sem(f"s_tabg{n}") for n in range(2)]
        s_tabs = [sem(f"s_tabs{n}") for n in range(2)]
        s_gath = [sem(f"s_gath{n}") for n in range(2)]
        s_XG, s_xgh, s_xgl, s_G, s_U, s_silu, s_h, s_HT, s_hTh, s_hTl, s_Y, s_y, s_add = (
            sem(f"s_{n}") for n in ("XG", "xgh", "xgl", "G", "U", "silu", "h", "HT", "hTh", "hTl", "Y", "y", "add"))

        x_v = x.rearrange("b (s p) d -> b p s d", p=P)
        c_v = ctx_in.rearrange("b (s p) d -> b p s d", p=P)
        w13_v = w13.rearrange("e (k p) f -> (e k) p f", p=P)
        w2_v = w2.rearrange("e (k p) d -> e p k d", p=P)
        rows_v = out[0:T].rearrange("(b s p) d -> b p s d", p=P, s=NS)
        xn_v = xn_dram[0:T].rearrange("(b s p) d -> b p s d", p=P, s=NS)

        def part(i):
            if not isinstance(i, int):
                return True, True, True, True
            return -1 <= i < B - 1, 0 <= i < B, 1 <= i <= B, 2 <= i <= B + 1

        def batches(engine, step, ahead=2):
            for i in range(-1, 3):
                step(i)
            with engine.Fori(3, B - ahead) as i:
                step(i)
            for i in range(B - ahead, B + 2):
                step(i)

        def entry_of(pp):
            if not isinstance(pp, int) or pp < 4:
                return 0, pp, 1
            turn = pp - 4
            return (turn + 1) % 2, turn // 2 + (0 if turn % 2 == 0 else 4), (5 if pp == 4 else 2)

        def half_rows(*buffers):
            return [buffer[:].rearrange("p a d -> p (a d)") for buffer in buffers]

        def w2_rows(e):
            return [w2_raw[:, (e * KF + at) * D:(e * KF + at + 2) * D] for at in (0, 2)]

        rooms = {1: w2_rows(NE - 1), 3: w2_rows(NE - 2), B + 3: half_rows(x_ln, c_turn),
                 B + 4: half_rows(bT, xnT), B + 5: half_rows(qT, cT), B + 6: half_rows(c_val, pT)}
        assert NE * KD == B + 8

        def through_raw(n):
            return n - (sum(n > m for m in rooms) if isinstance(n, int) else 2)

        def room_of(n):
            return s_rooms[list(rooms).index(n)]

        def halves_of(n):
            if isinstance(n, int) and n in rooms:
                return [(room, c * F, F) for c, room in enumerate(rooms[n])]
            return [(w13_raw[:], 0, F2)]

        def blocks(engine, step):
            first, last = 3, NBLK - 4
            for b in range(first):
                step(0, b)
            with engine.Fori(0, (last - first) // 4) as i:
                for c in range(first, first + 4):
                    step(i * 2, c)
            for b in range(last, NBLK + 1):
                step(0, b)

        assert (NBLK - 7) % 4 == 0

        block = ctx.enter_context(nc.Block())

        @block.sync
        def _(sp):
            def kp(w):
                return w.rearrange("(k p) d -> p k d", p=P)

            def norm_operand(b):
                at_least(sp, s_xn, b)
                sp.dma_start(x_ln[:], x_v[b]).then_inc(s_xl, 16)

            def turn_operand(b):
                at_least(sp, s_CT, b)
                sp.dma_start(c_turn[:], c_v[b]).then_inc(s_cturn, 16)

            def raw(n):
                before = n
                while isinstance(n, int) and before - 1 in rooms:
                    before -= 1
                at_least(sp, s_lo, before)
                sp.dma_start(w13_raw[:], w13_v[n]).then_inc(s_raw, 16)

            def raw_in_rooms(n, *used):
                for semaphore, count in used:
                    sp.wait_ge(semaphore, count)
                for src, at, cols in halves_of(n):
                    sp.dma_start(src, w13_v[n][:, at:at + cols]).then_inc(room_of(n), 16)

            sp.dma_start(wq_sb[:], kp(wq)).then_inc(s_wq, 16)
            sp.dma_start(wk_sb[:], kp(wk)).then_inc(s_wk, 16)
            norm_operand(0)
            turn_operand(0)
            with nc.allow_non_contiguous_dma("three bias vectors turned into columns"):
                for n, b in enumerate((bq, bk, bv)):
                    sp.dma_start(bias_col[:, n, :], b.rearrange("(k p) -> p k", p=P)).then_inc(s_small, 16)
            sp.dma_start(bo_row, bo.rearrange("(a d) -> a d", a=1)).then_inc(s_small, 16)
            sp.dma_start(wo_sb[:], kp(wo)).then_inc(s_wo, 16)
            sp.dma_start(wv_sb[:], kp(wv)).then_inc(s_wv, 16)
            sp.dma_start(router_sb[:], kp(router)).then_inc(s_small, 16)
            raw(0)
            norm_operand(1)
            sp.wait_ge(s_pre, 1)
            sp.dma_start(xn_dram[T:T + P], zero_f).then_inc(s_zeroed, 16)
            sp.dma_start(out[T:T + P], zero_f).then_inc(s_zeroed, 16)
            sp.wait_ge(s_spare, 2)
            sp.dma_start(table[0:ROWS].rearrange("(p c) w -> p (c w)", p=P),
                         spare.rearrange("p c w -> p (c w)")).then_inc(s_filled, 16)
            sp.dma_start(table[ROWS:ROWS + P].rearrange("(a c) w -> a (c w)", a=1),
                         spare[0:1].rearrange("p c w -> p (c w)")).then_inc(s_filled, 16)
            turn_operand(1)
            sp.dma_start(c_val[:], c_v[0]).then_inc(s_cval, 16)
            raw_in_rooms(1)
            raw_in_rooms(3)
            raw(2)
            norm_operand(2)
            turn_operand(2)

            def step(i):
                nxt, cur, prev, prev2 = part(i)
                p = i - 1
                if cur and not (isinstance(i, int) and i == 0):
                    sp.wait_ge(s_Z, i)
                    sp.dma_start(c_val[:], c_v[i]).then_inc(s_cval, 16)
                if prev2:
                    sp.wait_ge(s_xn2, i - 1)
                    sp.dma_start(xn_v[i - 2], xn2[:]).then_inc(s_store_xn, 16)
                if not isinstance(i, int) or 1 <= i < B - 2:
                    turn_operand(i + 2)
                if cur:
                    sp.dma_start(w2_raw[:, bass.ds(i * (KF * D), KF * D)].rearrange("p (k d) -> p k d", k=KF),
                                 w2_v[i]).then_inc(s_w2, 16)
                if prev:
                    sp.wait_ge(s_x1, p + 1)
                    sp.dma_start(rows_v[p], x1[:]).then_inc(s_store_x1, 16)
                if cur:
                    if isinstance(i, int) and i == 0:
                        sp.wait_ge(s_zeroed, 32)
                        sp.wait_ge(s_filled, 32)
                    at_least(sp, s_x1, i)
                    sp.dma_start(x_res[:], x_v[i]).then_inc(s_xs, 16)
                if not isinstance(i, int) or 0 <= i < B - 3:
                    norm_operand(i + 3)
                if not isinstance(i, int) or 2 <= i < B - 1:
                    raw(i + 3)
                if isinstance(i, int) and i == 0:
                    raw(4)
                if isinstance(i, int) and i == B - 1:
                    raw_in_rooms(B + 3, (s_xn, B), (s_CT, B))
                    raw_in_rooms(B + 4, (s_Q, B))
                if isinstance(i, int) and i == B:
                    raw(B + 2)
                    raw_in_rooms(B + 5, (s_S, B))
                    raw_in_rooms(B + 6, (s_Z, B))

            batches(sp, step, ahead=3)
            raw(B + 7)

            def first_row(j, c):
                return sp.value_load(meta[0:1, 1, bass.ds(2 * j + c, 1)], min_val=0, max_val=ROWS)

            def rows_gather(j, c):
                r = first_row(j, c)
                sp.dma_start(tab_g[:, c % 2, :], table[bass.ds(r, P), :]).then_inc(s_tabg[c % 2], 16)

            def rows_scatter(j, c):
                r = first_row(j, c)
                sp.dma_start(tab_s[:, c % 2, :], table[bass.ds(r, P), :]).then_inc(s_tabs[c % 2], 16)

            sp.wait_ge(s_meta, 1)
            for q in range(2):
                sp.wait_ge(s_scat[q], 16 * NS * TOP * (entry_of(B - 1 - q)[1] + 1))
            rows_gather(0, 0)
            rows_gather(0, 1)

            def load_rows(j, c):
                b = 2 * j + c
                if not isinstance(b, int) or b + 2 < NBLK:
                    sp.wait_ge(s_gath[c % 2], 16 * (j + c // 2 + 1))
                    own(sp, s_sp_here)
                    rows_gather(j, c + 2)
                if not isinstance(b, int) or b < NBLK:
                    at_least(sp, s_add, 16 * (b - 1))
                    own(sp, s_sp_here)
                    rows_scatter(j, c)

            blocks(sp, load_rows)
            sp.wait_ge(s_add, 16 * NBLK)
            sp.wait_ge(s_store_x1, 16 * B)
            sp.wait_ge(s_zeroed, 32)

        @block.scalar
        def _(act):
            def folded(count, dst, src):
                act.wait_ge(s_fold, count)
                nc.scalar.activation(dst, src, ACT.Copy).then_inc(s_folded, 1)

            def high(n):
                if isinstance(n, int) and n in rooms:
                    act.wait_ge(room_of(n), 32)
                else:
                    act.wait_ge(s_raw, 16 * (through_raw(n) + 1))
                for src, at, cols in halves_of(n):
                    w = nc.scalar.activation(w13_hi[:, bass.ds(n * F2 + at, cols)], src, ACT.Copy)
                w.then_inc(s_hi, 1)

            def w2_high(e):
                for semaphore, count in ((s_w2, 16 * NE),) + (
                        ((s_PT, B), (s_XT, B), (s_prod, B)),
                        ((s_x1, B), (s_O, B)),
                        ((s_O, B), (s_x1, B), (s_prod, B)),
                        ((s_X2, B), (s_store_x1, 16 * B), (s_store_xn, 16 * B)),
                        ((s_lo, B + 4),),
                        ((s_lo, B + 5),),
                        ((s_lo, B + 6),),
                        ((s_lo, B + 7),),
                )[e]:
                    act.wait_ge(semaphore, count)
                at = bass.ds(e * (KF * D), KF * D)
                nc.scalar.activation(w2_hi[:, at], w2_raw[:, at], ACT.Copy).then_inc(s_w2hi, 1)

            def norm(which, dst, src):
                for s in range(NS):
                    w = nc.scalar.activation(dst[:, s, :], src[:, s, :], ACT.Identity, bias=nmr[:, which, s:s + 1],
                                             scale=rstd[:, which, s:s + 1])
                return w

            def norm_in(b):
                act.wait_ge(s_nmr1, b + 1)
                at_least(act, s_XT, b)
                at_least(act, s_prod, b)
                norm(0, xn, x_ln).then_inc(s_xn, 1)

            def row_sums(b):
                act.wait_ge(s_prod, b + 1)
                at_least(act, s_qbk, b)
                for s in range(NS):
                    nc.scalar.activation(prod[:, s, :], prod[:, s, :], ACT.Copy,
                                         accum_out=qsum[:, s:s + 1]).then_inc(s_qsum, 1)

            def gate_exp(b):
                act.wait_ge(s_gap, b + 1)
                nc.scalar.activation(egap[:], gap[:], ACT.Exp).then_inc(s_egap, 1)

            def second_norm(b):
                act.wait_ge(s_nmr2, b + 1)
                at_least(act, s_X2, b)
                at_least(act, s_store_xn, 16 * b)
                norm(1, xn2, x1).then_inc(s_xn2, 1)

            norm_in(0)
            folded(1, bT[:].rearrange("p k d -> p (k d)"), Z[:])

            def step(i):
                nxt, cur, prev, prev2 = part(i)
                last = isinstance(i, int) and i >= B - 1
                n, p, pp = i + 1, i - 1, i - 2
                more = not isinstance(i, int) or i < B - 2
                if prev2:
                    act.wait_ge(s_X2, pp + 1)
                    nc.scalar.activation(x2T[:].rearrange("p k d -> p (k d)"), PT[:], ACT.Copy).then_inc(s_x2T, 1)
                if isinstance(i, int) and i == B:
                    w2_high(0)
                    w2_high(1)
                    second_norm(p)
                if nxt:
                    act.wait_ge(s_XT, n + 1)
                    nc.scalar.activation(xnT[:].rearrange("p k d -> p (k d)"), X[:], ACT.Copy).then_inc(s_xnT, 1)
                if isinstance(i, int) and i == 1:
                    high(3)
                if cur:
                    act.wait_ge(s_nb, i + 1)
                    at_least(act, s_rinv, i)
                    for s in range(NS):
                        nc.scalar.activation(probs[:, s, :], SC[:, s * S:(s + 1) * S], ACT.Exp,
                                             bias=nbias[:, s:s + 1], scale=SCALE,
                                             accum_out=rowsum[:, s:s + 1]).then_inc(s_exp, 1)
                if nxt:
                    act.wait_ge(s_CT, n + 1)
                    nc.scalar.activation(cT[:].rearrange("p k d -> p (k d)"), C[:], ACT.Copy).then_inc(s_cT, 1)
                if not isinstance(i, int) or i == 0 or 2 <= i < B:
                    high(i + 2)
                if isinstance(i, int) and i == -1:
                    act.wait_ge(s_fold, 2)
                    nc.scalar.activation(small[:], M[:, 0:KD + 1], ACT.Copy).then_inc(s_small_out, 1)
                    folded(2, wbk[:], M[:, D:2 * D])
                    folded(3, woT[:].rearrange("p k d -> p (k d)"), PT[:])
                    high(0)
                    row_sums(0)
                if prev2 and not last:
                    gate_exp(pp)
                early = isinstance(i, int) and i < 2
                if nxt and not early:
                    row_sums(n)
                if cur:
                    act.wait_ge(s_PT, i + 1)
                    at_least(act, s_Z, i)
                    nc.scalar.activation(pT[:].rearrange("p k d -> p (k d)"), PT[:], ACT.Copy).then_inc(s_pT, 1)
                if isinstance(i, int) and i == 0:
                    folded(5, bvo[:], O[:, 0:D])
                if nxt and early and cur:
                    row_sums(n)
                if nxt:
                    if isinstance(i, int) and i == -1:
                        act.wait_ge(s_small_out, 1)
                    act.wait_ge(s_Q, n + 1)
                    for m in range(KD):
                        nc.scalar.activation(qT[:, m, :], Q[:, m * S:(m + 1) * S], ACT.Identity,
                                             bias=small[:, m:m + 1]).then_inc(s_qT, 1)
                if more:
                    norm_in(i + 2)
                if isinstance(i, int) and i == -1:
                    folded(4, mvo[:].rearrange("p k d -> p (k d)"), O[:])
                    high(1)
                if prev and cur and not last:
                    second_norm(p)
                if cur and last:
                    gate_exp(pp)
                if cur:
                    act.wait_ge(s_Z, i + 1)
                    nc.scalar.activation(zT[:].rearrange("p k d -> p (k d)"), Z[:], ACT.Copy).then_inc(s_zT, 1)
                if cur and last:
                    second_norm(p)
                if isinstance(i, int) and i == B + 1:
                    high(B + 2)
                    high(B + 3)
                if last and not cur:
                    gate_exp(pp)

            batches(act, step)
            for n in (4, 5, 6):
                high(B + n)
            w2_high(2)
            high(B + 7)
            for e in range(3, NE):
                w2_high(e)

            def expert(j, c):
                b = 2 * j + c
                cur = not isinstance(b, int) or b < NBLK
                nxt = not isinstance(b, int) or b + 1 < NBLK
                if not isinstance(b, int) or b >= 1:
                    act.wait_ge(s_HT, b)
                    at_least(act, s_Y, b - 1)
                    nc.scalar.activation(hT_hi[:].rearrange("p k c -> p (k c)"), HT[:], ACT.Copy).then_inc(s_hTh, 1)
                if cur:
                    act.wait_ge(s_G, b + 1)
                    at_least(act, s_HT, b)
                    nc.scalar.activation(h[:], G[:], ACT.Silu).then_inc(s_silu, 1)
                if nxt:
                    act.wait_ge(s_XG, b + 2)
                    nc.scalar.activation(xgT_hi[:].rearrange("p k d -> p (k d)"), XG[:, 0:D], ACT.Copy).then_inc(s_xgh, 1)
                if not isinstance(b, int) or b >= 1:
                    act.wait_ge(s_Y, b)
                    act.wait_ge(s_tabs[(c + 1) % 2], 16 * (j + (c - 1) // 2 + 1))
                    at_least(act, s_add, 16 * (b - 2))
                    q = (c + 1) % 2
                    nc.scalar.activation(y[:, q, :], Y[:, 0:D], ACT.Copy,
                                         scale=tab_s[:, q, 1:2].bitcast(F32)).then_inc(s_y, 1)

            act.wait_ge(s_XG, 1)
            nc.scalar.activation(xgT_hi[:].rearrange("p k d -> p (k d)"), XG[:, 0:D], ACT.Copy).then_inc(s_xgh, 1)
            blocks(act, expert)

        @block.gpsimd
        def _(pool):
            g = nc.gpsimd
            g.memset(ident[:], 0.0).then_inc(s_const, 1)
            g.memset(before[:], 1.0).then_inc(s_const, 1)
            pool.wait_ge(s_const, 2)
            g.affine_select(out=ident[:], in_=ident[:], compare_op=ALU.not_equal, fill=1.0, base=0,
                            pattern=[[-1, P]], channel_multiplier=1).then_inc(s_const, 1)
            g.affine_select(out=before[:], in_=before[:], compare_op=ALU.is_gt, fill=0.0, base=0,
                            pattern=[[1, P]], channel_multiplier=-1).then_inc(s_const, 1)
            g.iota(spare[:, :, 0], [[1, P]], base=T, channel_multiplier=0).then_inc(s_spare, 1)
            g.memset(spare[:, :, 1], 0).then_inc(s_spare, 1)
            kw = dict(channel_multiplier=0, allow_small_or_imprecise_dtypes=True)
            g.iota(expert_no[:], [[0, NS], [0, TOP], [1, NE]], base=0, **kw).then_inc(s_const, 1)
            g.iota(expert_row[:], [[0, NS], [T, NE]], base=0, **kw).then_inc(s_const, 1)
            g.iota(block_edge[:], [[0, NE], [P, T // P]], base=0, **kw).then_inc(s_const, 1)
            g.iota(block_no[:], [[1, NMETA], [0, NE]], base=0, **kw).then_inc(s_const, 1)
            g.iota(entry[:, 0, :, :, 0], [[P, NS], [0, TOP]], base=-S, channel_multiplier=1).then_inc(s_tok, 1)
            g.iota(entry[:, 1, :, :, 0], [[P, NS], [0, TOP]], base=-S, channel_multiplier=1).then_inc(s_tok, 1)

            def rstd_of(which, s_in, s_eps, s_out, count):
                pool.wait_ge(s_in, count)
                own(pool, s_pool_here)
                g.tensor_scalar(var_eps[:, which, :], mv[:, which, :, 1], EPS, None, ALU.add).then_inc(s_eps, 1)
                pool.wait_ge(s_eps, count)
                g.tensor_tensor(rstd[:, which, :], var_eps[:, which, :], minus_half[:], ALU.pow).then_inc(s_out, 1)

            def rstd_in(b):
                rstd_of(0, s_st1, s_ve1, s_rs1, b + 1)

            def scatter(b, tiles):
                q = entry_of(b)[0]
                pool.wait_ge(s_tok, 2 * b + 3)
                pool.wait_ge(s_slot, b + 1)
                pool.wait_ge(s_w1, b + 1)
                own(pool, s_pool_here)
                for s in tiles:
                    for k in range(TOP):
                        g.indirect_dma_start(
                            out=table[:, :], out_offset=bass.IndirectOffsetOnAxis(ap=slot[:, q, s, k:k + 1], axis=0),
                            in_=entry[:, q, s, k, :], in_offset=None).then_inc(s_scat[q], 16)

            def times_wbk(b):
                pool.wait_ge(s_xn, b + 1)
                if isinstance(b, int) and b == 0:
                    pool.wait_ge(s_folded, 2)
                at_least(pool, s_qsum, NS * b)
                for s in range(NS):
                    w = g.tensor_tensor(prod[:, s, :], xn[:, s, :], wbk[:], ALU.mult)
                w.then_inc(s_prod, 1)

            pool.wait_ge(s_pre, 2)
            rstd_in(0)
            times_wbk(0)

            def step(i):
                nxt, cur, prev, prev2 = part(i)
                last = isinstance(i, int) and i >= B - 1
                n, p, pp = i + 1, i - 1, i - 2
                more = not isinstance(i, int) or i < B - 2
                if more:
                    rstd_in(i + 2)
                if prev:
                    rstd_of(1, s_st2, s_ve2, s_rs2, p + 1)
                if cur:
                    pool.wait_ge(s_xs, 16 * (i + 1))
                    if isinstance(i, int):
                        pool.wait_ge(s_folded, 5)
                    for s in range(NS):
                        g.tensor_tensor(x_res[:, s, :], x_res[:, s, :], bvo[:], ALU.add).then_inc(s_xb, 1)
                if more:
                    times_wbk(i + 2)
                if isinstance(i, int) and i == 1:
                    pool.wait_ge(s_filled, 32)
                if prev2 and isinstance(i, int) and i == B:
                    scatter(pp - 1, range(1, NS))
                if prev2:
                    scatter(pp, range(1 if last and cur else NS))

            batches(pool, step)

            def w2_low(e):
                pool.wait_ge(s_w2hi, e + 1)
                at = bass.ds(e * (KF * D), KF * D)
                g.tensor_tensor(w2_lo[:, at], w2_raw[:, at], w2_hi[:, at].bitcast(F32), ALU.subtract).then_inc(s_w2lo, 1)

            def gather(j, c):
                q = c % 2
                pool.wait_ge(s_tabg[q], 16 * (j + c // 2 + 1))
                own(pool, s_pool_here)
                g.indirect_dma_start(
                    out=xg[:, q, :], out_offset=None, in_=xn_dram[:, :],
                    in_offset=bass.IndirectOffsetOnAxis(ap=tab_g[:, q, 0:1], axis=0)).then_inc(s_gath[q], 16)

            w2_low(1)
            pool.wait_ge(s_store_xn, 16 * B)
            pool.wait_ge(s_store_x1, 16 * B)
            pool.wait_ge(s_zeroed, 32)
            gather(0, 0)
            gather(0, 1)
            w2_low(2)

            def expert(j, c):
                b = 2 * j + c
                if not isinstance(b, int) or b + 2 < NBLK:
                    pool.wait_ge(s_XG, b + 1)
                    gather(j, c + 2)
                if not isinstance(b, int) or b >= 1:
                    q = (c + 1) % 2
                    pool.wait_ge(s_y, b)
                    at_least(pool, s_add, 16 * (b - 1))
                    own(pool, s_pool_here)
                    g.indirect_dma_start(
                        out=out[:, :], out_offset=bass.IndirectOffsetOnAxis(ap=tab_s[:, q, 0:1], axis=0),
                        in_=y[:, q, :], in_offset=None, compute_op=ALU.add).then_inc(s_add, 16)

            blocks(pool, expert)

        @block.vector
        def _(dve):
            v = nc.vector
            v.memset(zero_f, 0.0).then_inc(s_pre, 1)
            v.memset(ones_f[:], 1.0).then_inc(s_wide, 1)
            v.memset(ones_b[:], 1.0).then_inc(s_wide, 1)
            v.memset(so_far[:], 0.0).then_inc(s_acc, 1)
            v.memset(minus_half[:], -0.5).then_inc(s_pre, 1)

            def norm_stats(which, src, s_bn, s_out, count):
                for s in range(NS):
                    v.bn_stats(st[:, which, s, :], src(s)).then_inc(s_bn, 1)
                for s in range(NS):
                    dve.wait_ge(s_bn, NS * (count - 1) + s + 1)
                    own(dve, s_dve_here)
                    w = v.bn_aggr(mv[:, which, s, :], st[:, which, s, :])
                w.then_inc(s_out, 1)

            def norm_in_stats(b):
                dve.wait_ge(s_xl, 16 * (b + 1))
                at_least(dve, s_xn, b)
                norm_stats(0, lambda s: x_ln[:, s, :], s_bn1, s_st1, b + 1)

            def minus_mean(which, s_rs, s_out, b):
                dve.wait_ge(s_rs, b + 1)
                v.scalar_tensor_tensor(out=nmr[:, which, :], in0=mv[:, which, :, 0], scalar=-1.0, in1=rstd[:, which, :],
                                       op0=ALU.mult, op1=ALU.mult).then_inc(s_out, 1)

            norm_in_stats(0)
            minus_mean(0, s_rs1, s_nmr1, 0)
            dve.wait_ge(s_small, 80)
            dve.wait_ge(s_wide, 2)
            for k in range(KD):
                v.tensor_scalar(bk_wide[:, k, :], ones_f[:], bias_col[:, 1, k:k + 1], None, ALU.mult).then_inc(s_wide, 1)
                v.tensor_scalar(bv_wide[:, k, :], ones_f[:], bias_col[:, 2, k:k + 1], None, ALU.mult).then_inc(s_wide, 1)

            def low(n):
                dve.wait_ge(s_hi, n + 1)
                for src, first, cols in halves_of(n):
                    at = bass.ds(n * F2 + first, cols)
                    w = v.tensor_tensor(w13_lo[:, at], src, w13_hi[:, at].bitcast(F32), ALU.subtract)
                w.then_inc(s_lo, 1)

            def w2_low(e):
                dve.wait_ge(s_w2hi, e + 1)
                at = bass.ds(e * (KF * D), KF * D)
                v.tensor_tensor(w2_lo[:, at], w2_raw[:, at], w2_hi[:, at].bitcast(F32), ALU.subtract).then_inc(s_w2lo, 1)

            def top_two(pp):
                dve.wait_ge(s_L, pp + 1)
                at_least(dve, s_topi, NS * pp)
                v.tensor_copy(logits[:].rearrange("p s e -> p (s e)"), M[:, 0:NS * NE]).then_inc(s_log, 1)
                dve.wait_ge(s_log, pp + 1)
                own(dve, s_dve_here)
                for s in range(NS):
                    v.max(top_v[:, s, :], logits[:, s, :]).then_inc(s_topv, 1)
                for s in range(NS):
                    dve.wait_ge(s_topv, NS * pp + s + 1)
                    own(dve, s_dve_here)
                    v.max_index(top_i[:, s, :], top_v[:, s, :], logits[:, s, :]).then_inc(s_topi, 1)
                v.tensor_tensor(gap[:], top_v[:, :, 1], top_v[:, :, 0], ALU.subtract).then_inc(s_gap, 1)

            def members(pp):
                dve.wait_ge(s_topi, NS * pp + NS)
                v.tensor_copy(top_f[:], top_i[:, :, 0:TOP]).then_inc(s_topf, 1)
                dve.wait_ge(s_topf, pp + 1)
                v.tensor_tensor(onehot[:], expert_no[:], top_f[:].unsqueeze(3).to_broadcast([P, NS, TOP, NE]),
                                ALU.is_equal).then_inc(s_hot, 1)
                dve.wait_ge(s_hot, pp + 1)
                at_least(dve, s_acc, NS * pp + 1)
                v.tensor_tensor(member[:], onehot[:, :, 0, :], onehot[:, :, 1, :], ALU.add).then_inc(s_mem, 1)

            def rows(pp):
                dve.wait_ge(s_POS, pp + 1)
                v.tensor_tensor(pos[:].rearrange("p s e -> p (s e)"), M[:, 64:64 + NS * NE],
                                expert_row[:].rearrange("p s e -> p (s e)"), ALU.add).then_inc(s_pos, 1)
                dve.wait_ge(s_acc, NS * pp + 1)
                v.tensor_tensor(so_far[:], so_far[:], member[:, 0, :], ALU.add).then_inc(s_acc, 1)
                dve.wait_ge(s_pos, pp + 1)
                for k in range(TOP):
                    w = v.tensor_tensor(picked[:, :, k, :], onehot[:, :, k, :], pos[:], ALU.mult)
                w.then_inc(s_pick, 1)
                dve.wait_ge(s_acc, NS * pp + 2)
                v.tensor_tensor(so_far[:], so_far[:], member[:, 1, :], ALU.add).then_inc(s_acc, 1)
                dve.wait_ge(s_egap, pp + 1)
                v.tensor_scalar(egap1[:], egap[:], 1.0, None, ALU.add).then_inc(s_eg1, 1)
                dve.wait_ge(s_pick, pp + 1)
                v.tensor_reduce(slot_f[:], picked[:], AX_X, ALU.add).then_inc(s_slotf, 1)
                q, before_this, back = entry_of(pp)
                at_least(dve, s_scat[q], 16 * NS * TOP * before_this)
                dve.wait_ge(s_tok, 2 * pp + 2)
                v.tensor_scalar(entry[:, q, :, :, 0], entry[:, q, :, :, 0], float(S * back), None,
                                ALU.add).then_inc(s_tok, 2)
                dve.wait_ge(s_slotf, pp + 1)
                v.tensor_copy(slot[:, q], slot_f[:]).then_inc(s_slot, 1)
                dve.wait_ge(s_eg1, pp + 1)
                v.reciprocal(entry_f[:, q, :, 0, 1], egap1[:]).then_inc(s_w0, 1)
                dve.wait_ge(s_w0, pp + 1)
                v.tensor_tensor(entry_f[:, q, :, 1, 1], egap[:], entry_f[:, q, :, 0, 1], ALU.mult).then_inc(s_w1, 1)

            def step(i):
                nxt, cur, prev, prev2 = part(i)
                last = isinstance(i, int) and i >= B - 1
                n, p, pp = i + 1, i - 1, i - 2
                more = not isinstance(i, int) or i < B - 2
                if cur:
                    dve.wait_ge(s_S, i + 1)
                    at_least(dve, s_nb, i)
                    v.tensor_reduce(smax[:], SC[:].rearrange("p (s k) -> p s k", s=NS), AX_X, ALU.max).then_inc(s_max, 1)
                    dve.wait_ge(s_max, 2 * i + 1)
                    dve.wait_ge(s_qbk, i + 1)
                    v.scalar_tensor_tensor(out=full_max[:], in0=smax[:], scalar=SCALE, in1=qbk[:],
                                           op0=ALU.mult, op1=ALU.add).then_inc(s_max, 1)
                    dve.wait_ge(s_max, 2 * i + 2)
                    at_least(dve, s_exp, NS * i)
                    v.tensor_tensor(nbias[:], qbk[:], full_max[:], ALU.subtract).then_inc(s_nb, 1)
                if isinstance(i, int) and i == 0:
                    low(1)
                if more:
                    norm_in_stats(i + 2)
                if isinstance(i, int) and i == 0:
                    low(i + 2)
                if prev2 and not (last and prev):
                    top_two(pp)
                    members(pp)
                if prev:
                    dve.wait_ge(s_O, p + 1)
                    dve.wait_ge(s_xb, NS * (p + 1))
                    dve.wait_ge(s_rinv, p + 1)
                    at_least(dve, s_store_x1, 16 * p)
                    at_least(dve, s_xn2, p)
                    for s in range(NS):
                        w = v.scalar_tensor_tensor(out=x1[:, s, :], in0=O[:, s * D:(s + 1) * D], scalar=rinv[:, s:s + 1],
                                                   in1=x_res[:, s, :], op0=ALU.mult, op1=ALU.add)
                    w.then_inc(s_x1, 1)
                if nxt:
                    dve.wait_ge(s_qsum, NS * (n + 1))
                    if isinstance(i, int) and i == -1:
                        dve.wait_ge(s_small_out, 1)
                    at_least(dve, s_nb, n)
                    v.tensor_scalar(qbk[:], qsum[:], small[:, KD:KD + 1], SCALE, ALU.add, ALU.mult).then_inc(s_qbk, 1)
                if prev:
                    dve.wait_ge(s_x1, p + 1)
                    norm_stats(1, lambda s: x1[:, s, :], s_bn2, s_st2, p + 1)
                if more:
                    minus_mean(0, s_rs1, s_nmr1, i + 2)
                if cur:
                    dve.wait_ge(s_exp, NS * (i + 1))
                    at_least(dve, s_x1, i)
                    v.reciprocal(rinv[:], rowsum[:]).then_inc(s_rinv, 1)
                if not isinstance(i, int) or 2 <= i < B - 1:
                    low(i + 2)
                if last and prev:
                    top_two(pp)
                if prev:
                    minus_mean(1, s_rs2, s_nmr2, p)
                if last and prev:
                    members(pp)
                if isinstance(i, int) and i in (1, B - 1):
                    low(i + 2)
                if prev2:
                    rows(pp)
                if isinstance(i, int) and i == B:
                    w2_low(0)
                if isinstance(i, int) and i == -1:
                    low(0)

            batches(dve, step)

            def link(ins, n):
                ins.then_inc(s_m, 1)
                dve.wait_ge(s_m, n)

            low(B + 2)
            dve.wait_ge(s_CNT, 1)
            link(v.tensor_copy(cnt[:], M[:, 0:NE]), 1)
            link(v.tensor_tensor(over, cnt[:].unsqueeze(2).to_broadcast([P, NE, T // P]), block_edge[:], ALU.is_gt), 2)
            link(v.tensor_reduce(nblk[:], over, AX_X, ALU.add), 3)
            link(v.tensor_tensor_scan(ends[:], ones_f[:, 0:NE], nblk[:], 0.0, ALU.mult, ALU.add), 4)
            link(v.tensor_tensor(done, block_no[:], ends[:].unsqueeze(1).to_broadcast([P, NMETA, NE]), ALU.is_ge), 5)
            link(v.tensor_reduce(blk_e[:], done, AX_X, ALU.add), 6)
            link(v.tensor_tensor(done, done, nblk[:].unsqueeze(1).to_broadcast([P, NMETA, NE]), ALU.mult), 7)
            link(v.tensor_reduce(blk_s[:], done, AX_X, ALU.add), 8)
            link(v.tensor_tensor(blk_s[:], block_no[:, :, 0], blk_s[:], ALU.subtract), 9)
            link(v.tensor_scalar(blk_s[:], blk_s[:], float(P), None, ALU.mult), 10)
            link(v.scalar_tensor_tensor(out=blk_r[:], in0=blk_e[:], scalar=float(T), in1=blk_s[:],
                                        op0=ALU.mult, op1=ALU.add), 11)
            link(v.tensor_scalar(meta[:, 0, :], blk_e[:], float(NE - 1), None, ALU.min), 12)
            v.tensor_scalar(meta[:, 1, :], blk_r[:], float(ROWS), None, ALU.min).then_inc(s_meta, 1)
            for n in range(3, 8):
                low(B + n)
            w2_low(3)

            def tokens_low(b):
                dve.wait_ge(s_xgh, b + 1)
                v.tensor_tensor(xgT_lo[:].rearrange("p k d -> p (k d)"), XG[:, 0:D],
                                xgT_hi[:].rearrange("p k d -> p (k d)").bitcast(F32), ALU.subtract).then_inc(s_xgl, 1)

            tokens_low(0)
            w2_low(4)
            w2_low(5)
            w2_low(6)

            def expert(j, c):
                b = 2 * j + c
                if not isinstance(b, int) or b < NBLK:
                    dve.wait_ge(s_silu, b + 1)
                    dve.wait_ge(s_U, b + 1)
                    v.tensor_tensor(h[:], h[:], U[:], ALU.mult).then_inc(s_h, 1)
                    if not isinstance(b, int) or b + 1 < NBLK:
                        tokens_low(b + 1)
                    if isinstance(b, int) and b == 0:
                        w2_low(7)
                    dve.wait_ge(s_hTh, b + 1)
                    v.tensor_tensor(hT_lo[:].rearrange("p k c -> p (k c)"), HT[:],
                                    hT_hi[:].rearrange("p k c -> p (k c)").bitcast(F32), ALU.subtract).then_inc(s_hTl, 1)

            blocks(dve, expert)

        @block.tensor
        def _(pe):
            t = nc.tensor

            def turned(dst, src, cols):
                for s in range(src.shape[1]):
                    for k in range(cols):
                        w = t.transpose(dst[:, k * src.shape[1] * P + s * P:k * src.shape[1] * P + (s + 1) * P],
                                        src[:, s, k * P:(k + 1) * P], ident[:])
                return w

            def fold_biases():
                pe.wait_ge(s_small, 80)
                pe.wait_ge(s_wide, 6)
                for m in range(KD):
                    for k in range(KD):
                        t.matmul(M[:, m:m + 1], wk_sb[:, k, m * P:(m + 1) * P], bias_col[:, 0, k:k + 1],
                                 start=(k == 0), stop=(k == KD - 1))
                for k in range(KD):
                    t.matmul(M[:, KD:KD + 1], bk_wide[:, k, :], bias_col[:, 0, k:k + 1],
                             start=(k == 0), stop=(k == KD - 1))
                for k in range(KD):
                    w = t.matmul(M[:, D:2 * D], bk_wide[:, k, :], wq_sb[:, k, :], start=(k == 0), stop=(k == KD - 1))
                w.then_inc(s_fold, 1)

            def turn_wo():
                pe.wait_ge(s_const, 4)
                pe.wait_ge(s_wo, 16)
                turned(PT, wo_sb, KD).then_inc(s_fold, 1)

            def fold_values():
                pe.wait_ge(s_wv, 16)
                pe.wait_ge(s_folded, 3)
                for m in range(KD):
                    for k in range(KD):
                        w = t.matmul(O[:, m * D:(m + 1) * D], wv_sb[:, k, m * P:(m + 1) * P], woT[:, k, :],
                                     start=(k == 0), stop=(k == KD - 1))
                w.then_inc(s_fold, 1)

            def fold_value_bias():
                pe.wait_ge(s_folded, 4)
                for k in range(KD):
                    t.matmul(O[:, 0:D], bv_wide[:, k, :], woT[:, k, :], start=(k == 0), stop=False)
                t.matmul(O[:, 0:D], ones_f[0:1, :], bo_row, start=False, stop=True).then_inc(s_fold, 1)

            def keep_busy(bank, times):
                with pe.Fori(0, times // 8):
                    for _ in range(8):
                        t.matmul(bank[:, 0:P], ones_b[:], ones_b[:], start=True, stop=True)

            pe.wait_ge(s_wide, 2)
            keep_busy(SC, 24)
            pe.wait_ge(s_const, 4)
            pe.wait_ge(s_wq, 16)
            pe.wait_ge(s_wk, 16)
            for m in range(KD):
                for k in range(KD):
                    w = t.matmul(Z[:, m * D:(m + 1) * D], wq_sb[:, k, m * P:(m + 1) * P], wk_sb[:, k, :],
                                 start=(k == 0), stop=(k == KD - 1))
            w.then_inc(s_fold, 1)

            def turn_second(b):
                pe.wait_ge(s_xn2, b + 1)
                if not isinstance(b, int) or b + 1 < B:
                    pe.wait_ge(s_pT, b + 2)
                turned(PT, xn2, KD).then_inc(s_X2, 1)

            def ranks(b):
                pe.wait_ge(s_mem, b + 1)
                pe.wait_ge(s_log, b + 1)
                pe.wait_ge(s_acc, NS * b + 1)
                for s in range(NS):
                    o = M[:, 64 + s * NE:64 + (s + 1) * NE]
                    t.matmul(o, before[:], member[:, s, :], start=True, stop=False)
                    w = t.matmul(o, ones_b[:], so_far[:], start=False, stop=(s == 0))
                    if s == 1:
                        w = t.matmul(o, ones_b[:], member[:, 0, :], start=False, stop=True)
                w.then_inc(s_POS, 1)

            def router_logits(b):
                pe.wait_ge(s_x2T, b + 1)
                at_least(pe, s_pos, b)
                for s in range(NS):
                    for k in range(KD):
                        w = t.matmul(M[:, s * NE:(s + 1) * NE], x2T[:, k, s * P:(s + 1) * P], router_sb[:, k, :],
                                     start=(k == 0), stop=(k == KD - 1))
                w.then_inc(s_L, 1)

            def step(i):
                nxt, cur, prev, prev2 = part(i)
                last = isinstance(i, int) and i >= B - 1
                n, p, pp = i + 1, i - 1, i - 2
                if cur:
                    pe.wait_ge(s_qT, KD * (i + 1))
                    pe.wait_ge(s_cT, i + 1)
                    at_least(pe, s_exp, NS * i)
                    for s in range(NS):
                        for k in range(KD):
                            w = t.matmul(SC[:, s * S:(s + 1) * S], qT[:, k, s * P:(s + 1) * P], cT[:, k, :],
                                         start=(k == 0), stop=(k == KD - 1))
                    w.then_inc(s_S, 1)
                if prev2 and not (isinstance(i, int) and i == B):
                    turn_second(pp)
                if nxt:
                    pe.wait_ge(s_xn, n + 1)
                    at_least(pe, s_xnT, n)
                    turned(X, xn, KD).then_inc(s_XT, 1)
                    pe.wait_ge(s_cturn, 16 * (n + 1))
                    turned(C, c_turn, KD).then_inc(s_CT, 1)
                if isinstance(i, int) and i == 0:
                    fold_value_bias()
                if isinstance(i, int) and i == -1:
                    fold_biases()
                    turn_wo()
                if prev2 and not last:
                    router_logits(pp)
                if prev:
                    if isinstance(i, int) and i == 1:
                        pe.wait_ge(s_folded, 5)
                    pe.wait_ge(s_zT, p + 1)
                    at_least(pe, s_x1, p)
                    for s in range(NS):
                        for k in range(KD):
                            w = t.matmul(O[:, s * D:(s + 1) * D], zT[:, k, s * P:(s + 1) * P], mvo[:, k, :],
                                         start=(k == 0), stop=(k == KD - 1))
                    w.then_inc(s_O, 1)
                if isinstance(i, int) and i == B:
                    turn_second(pp)
                if last and not prev:
                    keep_busy(SC, 16)
                if last:
                    router_logits(pp)
                if last and prev and not cur:
                    keep_busy(SC, 40)

                def project(m):
                    for k in range(KD):
                        w = t.matmul(Q[:, m * S:(m + 1) * S], bT[:, k, m * P:(m + 1) * P], xnT[:, k, :],
                                     start=(k == 0), stop=(k == KD - 1))
                    return w

                if nxt:
                    if isinstance(i, int) and i == -1:
                        pe.wait_ge(s_folded, 2)
                    pe.wait_ge(s_xnT, n + 1)
                    project(0)
                if cur:
                    pe.wait_ge(s_exp, NS * (i + 1))
                    at_least(pe, s_pT, i)
                    turned(PT, probs, NS).then_inc(s_PT, 1)
                if nxt:
                    project(1).then_inc(s_Q, 1)
                if isinstance(i, int) and i == -1:
                    fold_values()
                if prev2 and not (last and cur):
                    ranks(pp)
                if last and prev and not cur:
                    keep_busy(SC, 16)
                if cur:
                    pe.wait_ge(s_pT, i + 1)
                    pe.wait_ge(s_cval, 16 * (i + 1))
                    for m in range(KD):
                        for k in range(NS):
                            w = t.matmul(Z[:, m * S:(m + 1) * S], c_val[:, k, m * P:(m + 1) * P], pT[:, k, :],
                                         start=(k == 0), stop=(k == NS - 1))
                    w.then_inc(s_Z, 1)
                if last and cur:
                    ranks(pp)

            batches(pe, step)

            pe.wait_ge(s_acc, NS * B + 1)
            t.matmul(M[:, 0:NE], ones_b[:], so_far[:], start=True, stop=True).then_inc(s_CNT, 1)

            def turn_tokens(j, c):
                pe.wait_ge(s_gath[c % 2], 16 * (j + c // 2 + 1))
                for k in range(KD):
                    w = t.transpose(XG[:, k * P:(k + 1) * P], xg[:, c % 2, k * P:(k + 1) * P], ident[:])
                w.then_inc(s_XG, 1)

            def weights_of(j, c):
                e = pe.value_load(meta[0:1, 0, bass.ds(2 * j + c, 1)], min_val=0, max_val=NE - 1)
                return e * (KD * F2), e * (KF * D)

            pe.wait_ge(s_meta, 1)
            for q in range(2):
                pe.wait_ge(s_scat[q], 16 * NS * TOP * (entry_of(B - 1 - q)[1] + 1))
            first_at = weights_of(0, 0)[0]
            keep_busy(SC, 64)
            turn_tokens(0, 0)
            keep_busy(SC, 24)
            pe.wait_ge(s_lo, NE * KD)

            def up(dst, w13_at, column):
                first = True
                for x_part, w_part in ((xgT_hi, w13_hi), (xgT_hi, w13_lo), (xgT_lo, w13_hi)):
                    for k in range(KD):
                        w = t.matmul(dst[:], x_part[:, k, :], w_part[:, bass.ds(w13_at + (k * F2 + column), F)],
                                     start=first, stop=(x_part is xgT_lo and k == KD - 1))
                        first = False
                return w

            def expert(j, c):
                b = 2 * j + c
                cur = not isinstance(b, int) or b < NBLK
                if cur:
                    w13_at = first_at if isinstance(b, int) and b == 0 else weights_of(j, c)[0]
                if not isinstance(b, int) or b >= 1:
                    w2_at = weights_of(j, c - 1)[1]
                    pe.wait_ge(s_h, b)
                    for k in range(KF):
                        w = t.transpose(HT[:, k * P:(k + 1) * P], h[:, k * P:(k + 1) * P], ident[:])
                    w.then_inc(s_HT, 1)
                if cur:
                    pe.wait_ge(s_xgl, b + 1)
                    at_least(pe, s_silu, b)
                    up(G, w13_at, 0).then_inc(s_G, 1)
                    at_least(pe, s_h, b)
                    up(U, w13_at, F).then_inc(s_U, 1)
                if not isinstance(b, int) or b + 1 < NBLK:
                    turn_tokens(j, c + 1)
                if not isinstance(b, int) or b >= 1:
                    pe.wait_ge(s_hTh, b)
                    at_least(pe, s_y, b - 1)
                    if isinstance(b, int) and b == 1:
                        pe.wait_ge(s_w2lo, NE)
                    for n, (h_part, w_part) in enumerate(((hT_hi, w2_hi), (hT_hi, w2_lo), (hT_lo, w2_hi))):
                        if h_part is hT_lo:
                            pe.wait_ge(s_hTl, b)
                        for k in range(KF):
                            w = t.matmul(Y[:, 0:D], h_part[:, k, :], w_part[:, bass.ds(w2_at + k * D, D)],
                                         start=(n == 0 and k == 0), stop=(n == 2 and k == KF - 1))
                    w.then_inc(s_Y, 1)

            blocks(pe, expert)


_INS = ["x", "ctx_1024", "L0_xattn_Wq", "L0_xattn_bq", "L0_xattn_Wk", "L0_xattn_bk", "L0_xattn_Wv", "L0_xattn_bv",
        "L0_xattn_Wo", "L0_xattn_bo", "L0_ffn_moe_router", "L0_ffn_moe_w13", "L0_ffn_moe_w2"]


def kernel(**inputs):
    import numpy as _np
    import concourse.bacc as _bacc
    from concourse import mybir as _mybir
    from concourse.bass_utils import run_bass_kernel_spmd as _run

    nc = _bacc.Bacc("TRN2", target_bir_lowering=False, num_devices=1)
    arrays, args = {}, []
    for name in _INS:
        a = _np.ascontiguousarray(inputs[name])
        arrays[f"in_{name}_dram"] = a
        args.append(nc.dram_tensor(f"in_{name}_dram", a.shape, _mybir.dt.from_np(a.dtype), kind="ExternalInput").ap())
    shape = inputs["x"].shape
    tokens = shape[0] * shape[1]
    args.append(nc.dram_tensor("out_0_dram", (tokens + 128, shape[2]), _mybir.dt.float32, kind="ExternalOutput").ap())
    xattn_moe(nc, *args)
    r = _run(nc, [arrays], core_ids=[0])
    return r.results[0]["out_0_dram"][:tokens].reshape(shape)
```
